# Optimizing a Trainium2 kernel written in Bass

```python
import numpy as np
import jax
import jax.numpy as jnp

def _softmax(x, axis=-1):
    return jax.nn.softmax(x, axis=axis)

def _gelu(x):
    return jax.nn.gelu(x, approximate=True)

def _silu(x):
    return jax.nn.silu(x)

def _sigmoid(x):
    return jax.nn.sigmoid(x)

def _layernorm(x, axis=-1, eps=1e-05):
    m = jnp.mean(x, axis=axis, keepdims=True)
    v = jnp.var(x, axis=axis, keepdims=True)
    return (x - m) / jnp.sqrt(v + eps)

def _scatter_add(tgt, idx, src, axis=0):
    return tgt.at[idx].add(src)

def _segment_sum(src, seg, n):
    return jax.ops.segment_sum(src, seg, n)
kernel_name = 'mk_gnn_preln_d2_gnn_r8_315edd'

def setup_inputs(seed: int=0):
    np.random.seed(seed)
    _w = jnp.asarray

    def _rec_inputs():
        import jax
        import jax.numpy as jnp
        _gk = jax.random.key(seed)
        x = 0.0001712 + 1 * jax.random.normal(jax.random.fold_in(_gk, 1), (12500, 16), jnp.float32)
        _s = jax.random.randint(jax.random.fold_in(_gk, 2), (200000,), 0, 12500, jnp.int32)
        _d = jax.random.randint(jax.random.fold_in(_gk, 3), (200000,), 0, 12500, jnp.int32)
        _loop = jnp.arange(12500, dtype=jnp.int32)
        src = jnp.concatenate([_s, _d, _loop])
        dst = jnp.concatenate([_d, _s, _loop])
        _o = jnp.argsort(dst, stable=True)
        src = src[_o]
        dst = dst[_o]
        edge_attr_8 = 0.000714719 + 1.00021 * jax.random.normal(jax.random.fold_in(_gk, 12), (412500, 8), jnp.float32)
        edge_weight1 = jax.random.uniform(jax.random.fold_in(_gk, 14), (412500, 1), jnp.float32, 0.0, 1)
        return (x, src, dst, edge_attr_8, edge_weight1)
    x, src, dst, edge_attr_8, edge_weight1 = _rec_inputs()

    def _L0_gnn_setup():
        import jax, jax.numpy as jnp
        import numpy as np
        N_NODES = 6250
        N_EDGES = 50000
        D = 16
        E_FEAT = 8
        N_LAYERS = 3
        BN_EPS = 1e-05

        def _nnconv(x, src, dst, edge_attr, ew, eb, rw, rb):
            W = (edge_attr @ ew + eb).reshape(edge_attr.shape[0], x.shape[1], rw.shape[1])
            xj = x[src]
            msg = jnp.einsum('ei,eio->eo', xj, W)
            agg = jax.ops.segment_sum(msg, dst, num_segments=x.shape[0])
            return agg + x @ rw + rb

        def _batchnorm(x, gamma, beta):
            mean = jnp.mean(x, axis=0)
            var = jnp.mean(jnp.square(x - mean), axis=0)
            return (x - mean) * jax.lax.rsqrt(var + BN_EPS) * gamma + beta
        key = jax.random.key(seed)
        ks = jax.random.split(key, 12)
        x = jax.random.normal(ks[0], (N_NODES, D), dtype=jnp.float32)
        edge_index = jax.random.randint(ks[1], (2, N_EDGES), 0, N_NODES, dtype=jnp.int64)
        edge_attr = jax.random.normal(ks[2], (N_EDGES, E_FEAT), dtype=jnp.float32)
        s = 0.1
        edge_w = jax.random.normal(ks[3], (N_LAYERS, E_FEAT, D * D), dtype=jnp.float32) * s
        edge_b = jax.random.normal(ks[4], (N_LAYERS, D * D), dtype=jnp.float32) * s
        root_w = jax.random.normal(ks[5], (N_LAYERS, D, D), dtype=jnp.float32) * s
        root_b = jax.random.normal(ks[6], (N_LAYERS, D), dtype=jnp.float32) * s
        bn_gamma = jnp.ones((N_LAYERS - 1, D), dtype=jnp.float32)
        bn_beta = jnp.zeros((N_LAYERS - 1, D), dtype=jnp.float32)
        pred_w = jax.random.normal(ks[7], (D, D), dtype=jnp.float32) * s
        pred_b = jax.random.normal(ks[8], (D,), dtype=jnp.float32) * s
        return {'x': x, 'edge_index': edge_index, 'edge_attr': edge_attr, 'edge_w': edge_w, 'edge_b': edge_b, 'root_w': root_w, 'root_b': root_b, 'bn_gamma': bn_gamma, 'bn_beta': bn_beta, 'pred_w': pred_w, 'pred_b': pred_b}
    _L0_gnn_all = _L0_gnn_setup()
    _L0_gnn_in = {k: v for k, v in _L0_gnn_all.items() if k in ('edge_w', 'edge_b', 'root_w', 'root_b', 'bn_gamma', 'bn_beta', 'pred_w', 'pred_b')}
    del _L0_gnn_all

    def _L1_gnn_setup():
        import jax, jax.numpy as jnp
        import numpy as np
        N_NODES = 25000
        N_RAND_EDGES = 800000
        D = 16
        key = jax.random.key(seed)
        k1, k2, k3, k4, k5, k6 = jax.random.split(key, 6)
        inputs = jax.random.normal(k1, (N_NODES, D), dtype=jnp.float32)
        src_r = jax.random.randint(k2, (N_RAND_EDGES,), 0, N_NODES, dtype=jnp.int32)
        dst_r = jax.random.randint(k3, (N_RAND_EDGES,), 0, N_NODES, dtype=jnp.int32)
        loop = jnp.arange(N_NODES, dtype=jnp.int32)
        src = jnp.concatenate([src_r, loop])
        dst = jnp.concatenate([dst_r, loop])
        E = src.shape[0]
        timestamp = jax.random.uniform(k4, (E, 1), dtype=jnp.float32)
        W = jax.random.normal(k5, (D, D), dtype=jnp.float32) * (1.0 / np.sqrt(D))
        b = jax.random.normal(k6, (D,), dtype=jnp.float32) * 0.01
        return {'inputs': inputs, 'timestamp': timestamp, 'W': W, 'b': b, 'src': src, 'dst': dst}
    _L1_gnn_all = _L1_gnn_setup()
    _L1_gnn_in = {k: v for k, v in _L1_gnn_all.items() if k in ('W', 'b')}
    del _L1_gnn_all
    return {'x': x, 'src': src, 'dst': dst, 'edge_attr_8': edge_attr_8, 'edge_weight1': edge_weight1, 'L0_gnn_edge_w': _L0_gnn_in['edge_w'], 'L0_gnn_edge_b': _L0_gnn_in['edge_b'], 'L0_gnn_root_w': _L0_gnn_in['root_w'], 'L0_gnn_root_b': _L0_gnn_in['root_b'], 'L0_gnn_bn_gamma': _L0_gnn_in['bn_gamma'], 'L0_gnn_bn_beta': _L0_gnn_in['bn_beta'], 'L0_gnn_pred_w': _L0_gnn_in['pred_w'], 'L0_gnn_pred_b': _L0_gnn_in['pred_b'], 'L1_gnn_W': _L1_gnn_in['W'], 'L1_gnn_b': _L1_gnn_in['b']}

def reference(x, src, dst, edge_attr_8, edge_weight1, L0_gnn_edge_w, L0_gnn_edge_b, L0_gnn_root_w, L0_gnn_root_b, L0_gnn_bn_gamma, L0_gnn_bn_beta, L0_gnn_pred_w, L0_gnn_pred_b, L1_gnn_W, L1_gnn_b):
    import jax
    import jax.numpy as jnp

    def _L0_gnn_ref(x, edge_index, edge_attr, edge_w, edge_b, root_w, root_b, bn_gamma, bn_beta, pred_w, pred_b):
        import jax, jax.numpy as jnp
        import numpy as np
        N_NODES = 6250
        N_EDGES = 50000
        D = 16
        E_FEAT = 8
        N_LAYERS = 3
        BN_EPS = 1e-05

        def _nnconv(x, src, dst, edge_attr, ew, eb, rw, rb):
            W = (edge_attr @ ew + eb).reshape(edge_attr.shape[0], x.shape[1], rw.shape[1])
            xj = x[src]
            msg = jnp.einsum('ei,eio->eo', xj, W)
            agg = jax.ops.segment_sum(msg, dst, num_segments=x.shape[0])
            return agg + x @ rw + rb

        def _batchnorm(x, gamma, beta):
            mean = jnp.mean(x, axis=0)
            var = jnp.mean(jnp.square(x - mean), axis=0)
            return (x - mean) * jax.lax.rsqrt(var + BN_EPS) * gamma + beta
        src, dst = (edge_index[0], edge_index[1])
        h = x
        for i in range(N_LAYERS - 1):
            h = _nnconv(h, src, dst, edge_attr, edge_w[i], edge_b[i], root_w[i], root_b[i])
            h = _batchnorm(h, bn_gamma[i], bn_beta[i])
            h = jax.nn.relu(h)
        h = _nnconv(h, src, dst, edge_attr, edge_w[-1], edge_b[-1], root_w[-1], root_b[-1])
        h = jax.nn.relu(h)
        return h @ pred_w + pred_b

    def _L1_gnn_ref(inputs, timestamp, W, b, src, dst):
        import jax, jax.numpy as jnp
        import numpy as np
        N_NODES = 25000
        N_RAND_EDGES = 800000
        D = 16
        msg = inputs[src] * timestamp
        h = jax.ops.segment_max(msg, dst, num_segments=inputs.shape[0])
        return h @ W.T + b
    edge_index = jnp.stack([src, dst])
    h = jnp.maximum(_layernorm(x, axis=-1), 0.0)
    x = x + _L0_gnn_ref(h, edge_index, edge_attr_8, L0_gnn_edge_w, L0_gnn_edge_b, L0_gnn_root_w, L0_gnn_root_b, L0_gnn_bn_gamma, L0_gnn_bn_beta, L0_gnn_pred_w, L0_gnn_pred_b)
    h = jnp.maximum(_layernorm(x, axis=-1), 0.0)
    x = x + _L1_gnn_ref(h, edge_weight1, L1_gnn_W, L1_gnn_b, src, dst)
    return x

_drawn_inputs = setup_inputs


def setup_inputs(seed=0):
    import zlib

    import numpy as np

    out = dict(_drawn_inputs(seed))
    spreads = {'L0_gnn_bn_gamma': (1.0, 0.2), 'L0_gnn_bn_beta': (0.0, 0.1)}
    factors = {'L0_gnn_root_b': 7.875, 'L1_gnn_b': 8.0}
    for name, (base, spread) in spreads.items():
        noise = np.random.default_rng([zlib.crc32(name.encode()), seed]).standard_normal(out[name].shape)
        drawn = base * np.exp(spread * noise) if base else spread * noise
        out[name] = jnp.asarray(drawn.astype(out[name].dtype))
    for name, factor in factors.items():
        out[name] = (out[name] * factor).astype(out[name].dtype)
    return out
```

```python
import numpy as np
import concourse.bass as bass
from concourse import mybir
from contextlib import ExitStack

F32, BF16, I32 = mybir.dt.float32, mybir.dt.bfloat16, mybir.dt.int32
ALU = mybir.AluOpType
ACT = mybir.ActivationFunctionType
AX = mybir.AxisListType

P = 128
N, D, EF, E, LAYERS = 12500, 16, 8, 412500, 3
FB = EF + 1
ROW = FB * D
NB = -(-N // P)
NPAD = NB * P
LAST = N - (NB - 1) * P
T = 26
CHUNKS = 124
STREAM = T * CHUNKS
EPAD = P * STREAM
SLOTS = 2
GB = 7
GROUPS = NB // GB
CW = ROW + D
PER_BANK = 512 // CW
BIG = 1.5e38
LN_EPS = BN_EPS = 1e-5
assert EPAD >= E and E > (P - 1) * STREAM and GROUPS * GB == NB and GROUPS % SLOTS == 0
assert CHUNKS % SLOTS == 0


class Count:
    def __init__(self, sem):
        self.sem, self.n = sem, 0


def build(nc, io):
    ctx = ExitStack()

    def sb(name, shape, dt=F32):
        return ctx.enter_context(nc.sbuf_tensor(name, shape, dt))

    def sem(name):
        return Count(ctx.enter_context(nc.semaphore(name)))

    def slots(make, name, *a):
        return [make(f"{name}{s}", *a) for s in range(SLOTS)]

    with ctx:
        conv_table = nc.dram_tensor("conv_table", (NPAD, ROW), F32, kind="Internal").ap()
        max_table = nc.dram_tensor("max_table", (NPAD, D), F32, kind="Internal").ap()
        scanned = nc.dram_tensor("scanned", (EPAD, D), F32, kind="Internal").ap()
        conv_rows = conv_table.rearrange("(b p) c -> p b c", p=P)
        scanned_rows = scanned.rearrange("(p t) c -> p (t c)", p=P)

        src = sb("src", [P, STREAM], I32)
        dst = sb("dst", [P, STREAM], I32)
        same = sb("same", [P, STREAM])
        x = sb("x_res", [P, NB, D])
        h = sb("h", [P, NB, D])
        agg = sb("agg", [P, NB, D])
        root = sb("root", [P, NB, D])
        tmp = sb("tmp", [P, NB, D])
        ident = sb("ident", [P, P])
        upper = sb("upper", [P, P])
        ones = sb("ones", [P, P])
        lanes = sb("lanes", [P, P])
        real = sb("real", [P, 1])
        conv_w = sb("conv_w", [GB * D + 1, GB * CW])
        lin_w = sb("lin_w", [GB * D + 1, 2, GB * D])
        gamma = sb("gamma", [P, LAYERS - 1, D])
        beta = sb("beta", [P, LAYERS - 1, D])
        ends_i = sb("ends_i", [P, NB], I32)
        has = sb("has", [P, NB])
        cnt = sb("cnt", [P, NB])
        cum = sb("cum", [P, NB])
        tot = sb("tot", [P, NB])
        stat = sb("stat", [P, NB])
        stat2 = sb("stat2", [P, NB])
        bn = sb("bn", [P, 4, D])
        zeros = sb("zeros", [P, P], BF16)
        edge_i = sb("edge_i", [P, 4], I32)
        edge_m = sb("edge_m", [P, 6])
        head_lo = sb("head_lo", [P, P])
        head_hi = sb("head_hi", [P, NB])
        head_lo_i = sb("head_lo_i", [P, 2], I32)
        row_i = sb("row_i", [D, 3, P], I32)
        row_m = sb("row_m", [D, 6, P])
        state = sb("state", [P, D])
        state_row = sb("state_row", [D, P])
        carry_row = sb("carry_row", [D, P])
        carry = sb("carry", [P, D + 1])
        carry_hi = sb("carry_hi", [P, NB, D])

        idx = slots(sb, "idx", [P, T], I32)
        G = slots(sb, "gathered", [P, T, ROW])
        attr = slots(sb, "attr", [P, T, EF])
        msg = sb("msg", [P, T, D])
        run = slots(sb, "run", [P, T, D])
        dst_lo = slots(sb, "dst_lo", [P, T], I32)
        dst_hi = slots(sb, "dst_hi", [P, T], I32)
        hot_lo = slots(sb, "hot_lo", [P, T, P], BF16)
        hot_hi = slots(sb, "hot_hi", [P, T, NB], BF16)
        hs = slots(sb, "hs", [P, GB * D + 1])
        hT = slots(sb, "hT", [GB * D + 1, P])
        rows = slots(sb, "rows", [P, GB, ROW])

        pT = [ctx.enter_context(nc.psum_tensor(f"pT{s}", [P, 512], F32)) for s in range(SLOTS)]
        pY = [ctx.enter_context(nc.psum_tensor(f"pY{s}", [P, 3, 512], F32)) for s in range(SLOTS)]
        pC = pT[1]

        s_in = sem("s_in")
        s_w = sem("s_w")
        s_init = sem("s_init")
        s_free = slots(sem, "s_free")
        s_idx = slots(sem, "s_idx")
        s_run = slots(sem, "s_run")
        s_runfree = slots(sem, "s_runfree")
        s_step = sem("s_step")
        s_hot = slots(sem, "s_hot")
        s_hotfree = slots(sem, "s_hotfree")
        s_hs = slots(sem, "s_hs")
        s_tr = slots(sem, "s_tr")
        s_hT = slots(sem, "s_hT")
        s_mm = slots(sem, "s_mm")
        s_rows = slots(sem, "s_rows")
        s_rowsfree = slots(sem, "s_rowsfree")
        s_v = sem("s_v")
        s_p = sem("s_p")
        s_a = sem("s_a")
        s_tab = sem("s_tab")
        s_out = sem("s_out")
        tick = {e: sem(f"s_tick_{e}") for e in ("pool", "act", "dve", "pe", "sp")}

        programs = {e: [] for e in ("sync", "gpsimd", "scalar", "vector", "tensor")}

        def on(engine):
            return programs[engine].append

        def gate(eng, who, s, value):
            eng.wait_ge(s.sem, value)
            eng.sem_inc(tick[who].sem, 1)

        def bump(s, n=1):
            s.n += n
            return s.n

        loads = [(src, io["src"]), (dst, io["dst"]), (x, io["x"]), (ident, io["ident"]),
                 (upper, io["upper"]), (lanes, io["lanes"]), (real, io["real"]),
                 (lin_w, io["lin_w"]), (gamma, io["gamma"]), (beta, io["beta"]),
                 (edge_i, io["borders"]), (row_i, io["borders_row"]), (conv_w, io["conv_w"][0])]

        def sync_start(e):
            for tile, ap in loads:
                shape = list(tile.shape)
                e.dma_start(tile[tuple(slice(None) for _ in shape)], ap).then_inc(s_in.sem, 16)
        on("sync")(sync_start)
        bump(s_in, 16 * len(loads))
        IN_ALL = s_in.n

        def step(e, ins):
            ins.then_inc(s_step.sem, 1)
            s_step.n += 1
            e.wait_ge(s_step.sem, s_step.n)

        def tt(e, out, a, b, op):
            return e.tensor_tensor(out, a, b, op)

        INIT_ALL = 3 + 2 * SLOTS

        def vector_start(e):
            e.memset(ones[:, :], 1.0).then_inc(s_init.sem, 1)
            e.memset(zeros[:, :], 0.0).then_inc(s_init.sem, 1)
            for s in range(SLOTS):
                e.memset(hs[s][:, :], 1.0).then_inc(s_init.sem, 1)
                e.memset(run[s][:, :, :], 0.0).then_inc(s_init.sem, 1)
                e.memset(G[s][:, 0, 0:1], 0.0).then_inc(s_free[s].sem, 1)
            e.memset(carry[:, D:D + 1], 1.0).then_inc(s_init.sem, 1)
            e.wait_ge(s_in.sem, IN_ALL)
            e.wait_ge(s_init.sem, INIT_ALL)
            step(e, e.memset(same[:, 0:1], 0.0))
            e.tensor_tensor(same[:, 1:STREAM], dst[:, 1:STREAM], dst[:, 0:STREAM - 1], ALU.is_equal)
            first, last, prev_last, next_first = (edge_i[:, k:k + 1] for k in range(4))
            tt(e, edge_m[:, 0:1], first, prev_last, ALU.is_equal)
            tt(e, edge_m[:, 1:2], first, last, ALU.is_equal)
            step(e, tt(e, edge_m[:, 2:3], next_first, last, ALU.is_equal))
            step(e, tt(e, edge_m[:, 3:4], edge_m[:, 1:2], edge_m[:, 2:3], ALU.mult))
            step(e, e.tensor_scalar(edge_m[:, 4:5], edge_m[:, 3:4], -1.0, 1.0, ALU.mult, ALU.add))
            e.tensor_scalar(head_lo_i[:, 0:1], first, P - 1, None, ALU.bitwise_and)
            step(e, e.tensor_scalar(head_lo_i[:, 1:2], first, 7, None, ALU.logical_shift_right))
            step(e, e.tensor_copy(edge_m[:, 0:2], head_lo_i[:, 0:2]))
            step(e, e.tensor_scalar(head_lo[:, :], lanes[:, :], edge_m[:, 0:1], edge_m[:, 4:5],
                                    ALU.is_equal, ALU.mult))
            step(e, e.tensor_scalar(head_hi[:, :], lanes[:, 0:NB], edge_m[:, 1:2], None, ALU.is_equal))
            rf, rpl, rpf = (row_i[:, k, :] for k in range(3))
            tt(e, row_m[:, 0, :], rf, rpl, ALU.is_equal)
            step(e, tt(e, row_m[:, 1, :], rpf, rpl, ALU.is_equal))
            step(e, tt(e, row_m[:, 2, :], row_m[:, 0, :], row_m[:, 1, :], ALU.mult))
            e.tensor_scalar(row_m[:, 3, :], row_m[:, 0, :], BIG, -BIG, ALU.mult, ALU.add)
            step(e, e.tensor_scalar(row_m[:, 4, :], row_m[:, 2, :], BIG, -BIG, ALU.mult, ALU.add))
        on("vector")(vector_start)

        def credits(name, engine, counts):
            def f(e):
                for c in counts:
                    e.sem_inc(c.sem, 1)
            on(engine)(f)
            for c in counts:
                c.n = 1
        for c in s_free:
            c.n = 1
        credits("sp", "sync", s_runfree + s_rowsfree)
        credits("pe", "tensor", s_tr + s_mm + s_hotfree)
        credits("dve", "vector", s_rows)
        for c in s_rows:
            c.n = 1

        def spread(t):
            return t.unsqueeze(2).to_broadcast([P, NB, D])

        def norm_relu():
            a0 = s_a.n
            bump(s_a)
            bump(s_v)
            v0 = s_v.n

            def vec(e):
                step(e, e.tensor_reduce(stat[:, :], x[:, :, :], AX.X, ALU.add))
                step(e, e.tensor_scalar(stat[:, :], stat[:, :], 1.0 / D, None, ALU.mult))
                step(e, tt(e, h[:, :, :], x[:, :, :], spread(stat[:, :]), ALU.subtract))
                step(e, tt(e, tmp[:, :, :], h[:, :, :], h[:, :, :], ALU.mult))
                step(e, e.tensor_reduce(stat2[:, :], tmp[:, :, :], AX.X, ALU.add))
                e.tensor_scalar(stat2[:, :], stat2[:, :], 1.0 / D, LN_EPS, ALU.mult,
                                ALU.add).then_inc(s_v.sem, 1)
                e.wait_ge(s_a.sem, a0 + 1)
                step(e, e.reciprocal(stat2[:, :], stat[:, :]))
                step(e, tt(e, tmp[:, :, :], h[:, :, :], spread(stat2[:, :]), ALU.mult))
                step(e, e.tensor_scalar(h[:, :, :], tmp[:, :, :], 0.0, None, ALU.max))
            on("vector")(vec)

            def act(e):
                e.wait_ge(s_v.sem, v0)
                e.activation(stat[:, :], stat2[:, :], ACT.Sqrt).then_inc(s_a.sem, 1)
            on("scalar")(act)
            publish_h()

        def publish_h():
            bump(s_v)
            on("vector")(lambda e: e.tensor_copy(tmp[:, 0, 0:1], h[:, 0, 0:1]).then_inc(s_v.sem, 1))

        def node_product(weights, width, out_fn, store, wait_weights=None):
            v_ready = s_v.n
            b = {k: [c.n for c in cs] for k, cs in
                 dict(hs=s_hs, tr=s_tr, hT=s_hT, mm=s_mm, rows=s_rows, rf=s_rowsfree).items()}
            per_bank = 512 // width if width * GB > 512 else GB
            pieces = [(k, min(per_bank, GB - k)) for k in range(0, GB, per_bank)]
            store_sems = slots(sem, f"s_store{len(programs['sync'])}_") if store else None

            def act(e):
                e.wait_ge(s_v.sem, v_ready)
                with e.Fori(0, GROUPS // SLOTS) as i:
                    for s in range(SLOTS):
                        gate(e, "act", s_tr[s], i + b["tr"][s])
                        hf = h[:, :, :].rearrange("p b d -> p (b d)")
                        e.copy(hs[s][:, 0:GB * D],
                               hf[:, bass.ds((i * SLOTS + s) * GB * D, GB * D)]).then_inc(s_hs[s].sem, 1)
                    for s in range(SLOTS):
                        gate(e, "act", s_tr[s], i + b["tr"][s] + 1)
                        gate(e, "act", s_mm[s], i + b["mm"][s])
                        e.copy(hT[s][:, :], pT[s][0:GB * D + 1, 0:P]).then_inc(s_hT[s].sem, 1)
            on("scalar")(act)

            def pe(e):
                if wait_weights is not None:
                    e.wait_ge(wait_weights[0].sem, wait_weights[1])
                with e.Fori(0, GROUPS // SLOTS) as i:
                    for s in range(SLOTS):
                        gate(e, "pe", s_hs[s], i + b["hs"][s] + 1)
                        e.transpose(pT[s][0:GB * D + 1, 0:P], hs[s][:, :], ident[:, :]).then_inc(s_tr[s].sem, 1)
                    for s in range(SLOTS):
                        gate(e, "pe", s_hT[s], i + b["hT"][s] + 1)
                        gate(e, "pe", s_rows[s], i + b["rows"][s])
                        for n, (k, m) in enumerate(pieces):
                            ins = e.matmul(pY[s][:, n, 0:m * width], hT[s][:, :],
                                           weights[:, k * width:(k + m) * width], start=True, stop=True)
                        ins.then_inc(s_mm[s].sem, 1)
            on("tensor")(pe)

            def vec(e):
                with e.Fori(0, GROUPS // SLOTS) as i:
                    for s in range(SLOTS):
                        gate(e, "dve", s_mm[s], i + b["mm"][s] + 1)
                        if store:
                            gate(e, "dve", s_rowsfree[s], i + b["rf"][s])
                        for n, (k, m) in enumerate(pieces):
                            ps = pY[s][:, n, 0:m * width].rearrange("p (b c) -> p b c", c=width)
                            ins = out_fn(e, s, ps, i * SLOTS + s, k, m)
                        ins.then_inc(s_rows[s].sem, 1)
            on("vector")(vec)

            it = GROUPS // SLOTS
            if store:
                def sp(e):
                    with e.Fori(0, it) as i:
                        for s in range(SLOTS):
                            gate(e, "sp", s_rows[s], i + b["rows"][s] + 1)
                            e.dma_start(conv_rows[:, bass.ds((i * SLOTS + s) * GB, GB), :],
                                        rows[s][:, :, :]).then_inc(store_sems[s].sem, 16)
                        for s in range(SLOTS):
                            gate(e, "sp", store_sems[s], i * 16 + 16)
                            e.sem_inc(s_rowsfree[s].sem, 1)
                    e.sem_inc(s_tab.sem, 1)
                on("sync")(sp)
                bump(s_tab)
            for cs in (s_hs, s_tr, s_hT, s_mm, s_rows) + ((s_rowsfree,) if store else ()):
                for c in cs:
                    bump(c, it)

        def gather(name, indices, ready, table, width, steps, iters, vec_chunk, extra_ready=None):
            got = slots(sem, f"s_got_{name}")
            b_free, b_idx = [c.n for c in s_free], [c.n for c in s_idx]

            def act(e):
                for c, v in ready.get("act", ()):
                    e.wait_ge(c.sem, v)
                with e.Fori(0, iters) as i:
                    for s in range(SLOTS):
                        gate(e, "act", s_free[s], i + b_free[s])
                        e.copy(idx[s][:, 0:steps], indices[:, bass.ds((i * SLOTS + s) * steps, steps)]
                               ).then_inc(s_idx[s].sem, 1)
            on("scalar")(act)

            def pool(e):
                for c, v in ready.get("pool", ()):
                    e.wait_ge(c.sem, v)
                with e.Fori(0, iters) as i:
                    for s in range(SLOTS):
                        gate(e, "pool", s_idx[s], i + b_idx[s] + 1)
                        for t in range(steps):
                            e.indirect_dma_start(
                                out=G[s][:, t, 0:width], out_offset=None, in_=table[:, :],
                                in_offset=bass.IndirectOffsetOnAxis(ap=idx[s][:, t:t + 1], axis=0)
                            ).then_inc(got[s].sem, 16)
            on("gpsimd")(pool)

            def vec(e):
                base = s_step.n
                per = [0]

                def chain(ins):
                    ins.then_inc(s_step.sem, 1)
                    per[0] += 1
                    return per[0]
                with e.Fori(0, iters) as i:
                    PER = vec_chunk.steps * SLOTS

                    def order(ins):
                        k = chain(ins)
                        gate(e, "dve", s_step, base + i * PER + k)
                    for s in range(SLOTS):
                        gate(e, "dve", got[s], (i + 1) * (16 * steps))
                        vec_chunk(e, i, s, order)
                    assert per[0] == PER, (per[0], PER)
                s_step.n += PER * iters
            on("vector")(vec)
            for c in s_free + s_idx:
                bump(c, iters)

        def edges(name, table, width, attr_dram, attr_width, ready, is_max, count):
            iters = CHUNKS // SLOTS
            b_free, b_run, b_rf = ([c.n for c in cs] for cs in (s_free, s_run, s_runfree))
            b_hot, b_hf = ([c.n for c in cs] for cs in (s_hot, s_hotfree))
            loaded = slots(sem, f"s_attr_{name}")
            stored = slots(sem, f"s_stored_{name}")

            def sp(e):
                with e.Fori(0, iters) as i:
                    for s in range(SLOTS):
                        gate(e, "sp", s_free[s], i + b_free[s])
                        e.dma_start(attr[s][:, :, 0:attr_width].rearrange("p t f -> p (t f)")
                                    if attr_width == EF else attr1[s],
                                    attr_dram[:, bass.ds((i * SLOTS + s) * T * attr_width, T * attr_width)]
                                    ).then_inc(loaded[s].sem, 16)
                    for s in range(SLOTS):
                        gate(e, "sp", s_run[s], i + b_run[s] + 1)
                        e.dma_start(scanned_rows[:, bass.ds((i * SLOTS + s) * T * D, T * D)],
                                    run[s][:, :, :].rearrange("p t d -> p (t d)")).then_inc(stored[s].sem, 16)
                    for s in range(SLOTS):
                        gate(e, "sp", stored[s], i * 16 + 16)
                        e.sem_inc(s_runfree[s].sem, 1)
                e.sem_inc(s_tab.sem, 1)
            on("sync")(sp)
            bump(s_tab)

            def chunk(e, i, s, order):
                c = i * SLOTS + s
                gate(e, "dve", loaded[s], i * 16 + 16)
                g = G[s]
                if is_max:
                    tt(e, msg[:, :, :], g[:, :, 0:D], attr1[s].unsqueeze(2).to_broadcast([P, T, D]),
                       ALU.mult).then_inc(s_free[s].sem, 1)
                    order(e.memset(sink[:, :], 0.0))
                else:
                    g4 = g[:, :, 0:EF * D].rearrange("p t (f d) -> p t f d", d=D)
                    order(tt(e, g4, g4, attr[s][:, :, :].unsqueeze(3).to_broadcast([P, T, EF, D]), ALU.mult))
                    e.tensor_reduce(msg[:, :, :], g[:, :, :].rearrange("p t (f d) -> p t d f", d=D),
                                    AX.X, ALU.add).then_inc(s_free[s].sem, 1)
                    order(e.memset(sink[:, :], 0.0))
                gate(e, "dve", s_runfree[s], i + b_rf[s])
                flags = same[:, bass.ds(c * T, T)]
                for d in range(D):
                    ins = e.tensor_tensor_scan(run[s][:, :, d], flags, msg[:, :, d],
                                               run[1 - s][:, T - 1, d:d + 1],
                                               ALU.add if is_max else ALU.mult,
                                               ALU.max if is_max else ALU.add)
                ins.then_inc(s_run[s].sem, 1)
                order(e.memset(sink[:, :], 0.0))
                if count:
                    gate(e, "dve", s_hotfree[s], i + b_hf[s])
                    dchunk = dst[:, bass.ds(c * T, T)]
                    e.tensor_scalar(dst_lo[s][:, :], dchunk, P - 1, None, ALU.bitwise_and)
                    order(e.tensor_scalar(dst_hi[s][:, :], dchunk, 7, None, ALU.logical_shift_right))
                    tt(e, hot_lo[s][:, :, :], dst_lo[s][:, :].unsqueeze(2).to_broadcast([P, T, P]),
                       lanes[:, :].unsqueeze(1).to_broadcast([P, T, P]), ALU.is_equal)
                    tt(e, hot_hi[s][:, :, :], dst_hi[s][:, :].unsqueeze(2).to_broadcast([P, T, NB]),
                       lanes[:, 0:NB].unsqueeze(1).to_broadcast([P, T, NB]), ALU.is_equal
                       ).then_inc(s_hot[s].sem, 1)
            chunk.steps = (2 if is_max else 3) + (1 if count else 0)

            if count:
                def pe(e):
                    e.wait_ge(s_init.sem, INIT_ALL)
                    e.matmul(pC[:, 0:NB], zeros[:, :], zeros[:, 0:NB], start=True, stop=False,
                             skip_group_check=True).then_inc(s_p.sem, 1)
                    with e.Fori(0, iters) as i:
                        for s in range(SLOTS):
                            gate(e, "pe", s_hot[s], i + b_hot[s] + 1)
                            for t in range(T):
                                ins = e.matmul(pC[:, 0:NB], hot_lo[s][:, t, :], hot_hi[s][:, t, :],
                                               start=False, stop=False, skip_group_check=True)
                            ins.then_inc(s_hotfree[s].sem, 1)
                on("tensor")(pe)
                bump(s_p)
                for cc in s_hot + s_hotfree:
                    bump(cc, iters)

            gather(name, src, ready, table, width, T, iters, chunk)
            for cc in s_run + s_runfree:
                bump(cc, iters)

        attr1 = [a[:, :, :].rearrange("p t f -> p (t f)")[:, 0:T] for a in attr]
        sink = sb("sink", [P, 1])

        def hand_over_vec():
            v = bump(s_v)
            on("vector")(lambda e: e.memset(sink[:, :], 0.0).then_inc(s_v.sem, 1))
            return v

        def node_ends():
            p0, v0 = s_p.n, s_v.n
            hf = [c.n for c in s_hotfree]
            bump(s_p)
            bump(s_v, 2)

            def vec1(e):
                for s in range(SLOTS):
                    e.wait_ge(s_hotfree[s].sem, hf[s])
                e.tensor_copy(cnt[:, :], pC[:, 0:NB]).then_inc(s_v.sem, 1)
                e.wait_ge(s_p.sem, p0 + 1)
                step(e, e.tensor_copy(tot[:, :], pC[:, NB:2 * NB]))
                step(e, e.tensor_tensor_scan(cum[:, :], tot[:, :], tot[:, :], 0.0, ALU.add, ALU.max))
                step(e, tt(e, cum[:, :], cum[:, :], tot[:, :], ALU.subtract))
                step(e, tt(e, cum[:, :], cum[:, :], pC[:, 2 * NB:3 * NB], ALU.add))
                e.tensor_scalar(has[:, :], cnt[:, :], 1.0, None, ALU.min)
                step(e, e.tensor_scalar(cum[:, :], cum[:, :], -1.0, 0.0, ALU.add, ALU.max))
                e.tensor_copy(ends_i[:, :], cum[:, :]).then_inc(s_v.sem, 1)
            on("vector")(vec1)

            def pe(e):
                e.wait_ge(s_v.sem, v0 + 1)
                e.matmul(pC[:, NB:2 * NB], ones[:, :], cnt[:, :], start=True, stop=True)
                e.matmul(pC[:, 2 * NB:3 * NB], upper[:, :], cnt[:, :], start=True, stop=True
                         ).then_inc(s_p.sem, 1)
            on("tensor")(pe)
            return v0 + 2

        def nodes(name, is_max, ends_ready):
            run_last = run[(CHUNKS - 1) % SLOTS]
            run_v = s_run[(CHUNKS - 1) % SLOTS].n
            tab = s_tab.n
            p0, v0 = s_p.n, s_v.n
            bump(s_p, 3)
            bump(s_v, 3)

            def vec_carry(e):
                e.wait_ge(s_run[(CHUNKS - 1) % SLOTS].sem, run_v)
                e.tensor_copy(state[:, :], run_last[:, T - 1, :]).then_inc(s_v.sem, 1)
                e.wait_ge(s_p.sem, p0 + 1)
                step(e, e.memset(state_row[:, 0:1], -BIG if is_max else 0.0))
                if is_max:
                    step(e, tt(e, state_row[:, 1:P], pT[0][0:D, 0:P - 1], row_m[:, 0, 1:P], ALU.mult))
                    step(e, tt(e, state_row[:, 1:P], state_row[:, 1:P], row_m[:, 3, 1:P], ALU.add))
                    step(e, e.tensor_tensor_scan(carry_row[:, :], row_m[:, 4, :], state_row[:, :], -BIG,
                                                 ALU.add, ALU.max))
                else:
                    step(e, tt(e, state_row[:, 1:P], pT[0][0:D, 0:P - 1], row_m[:, 0, 1:P], ALU.mult))
                    step(e, e.tensor_tensor_scan(carry_row[:, :], row_m[:, 2, :], state_row[:, :], 0.0,
                                                 ALU.mult, ALU.add))
                e.memset(sink[:, :], 0.0).then_inc(s_v.sem, 1)
                e.wait_ge(s_p.sem, p0 + 2)
                step(e, e.tensor_copy(carry[:, 0:D], pT[1][:, 0:D]))
                e.tensor_tensor(carry_hi[:, :, :], head_hi[:, :].unsqueeze(2).to_broadcast([P, NB, D]),
                                carry[:, 0:D].unsqueeze(1).to_broadcast([P, NB, D]),
                                ALU.mult).then_inc(s_v.sem, 1)
            on("vector")(vec_carry)

            rows_b = [c.n for c in s_rows]

            def pe(e):
                e.wait_ge(s_v.sem, v0 + 1)
                e.transpose(pT[0][0:D, 0:P], state[:, :], ident[:, :]).then_inc(s_p.sem, 1)
                e.wait_ge(s_v.sem, v0 + 2)
                e.transpose(pT[1][:, 0:D], carry_row[:, :], ident[0:D, 0:D]).then_inc(s_p.sem, 1)
                e.wait_ge(s_v.sem, v0 + 3)
                for s in range(SLOTS):
                    e.wait_ge(s_rows[s].sem, rows_b[s])
                flat = carry_hi[:, :, :].rearrange("p b d -> p (b d)")
                w = NB * D // 4
                for k in range(4):
                    e.matmul(pY[k // 2][:, k % 2, 0:w], head_lo[:, :], flat[:, k * w:(k + 1) * w],
                             start=True, stop=True)
                e.matmul(pY[0][:, 2, 0:NB], head_lo[:, :], head_hi[:, :], start=True, stop=True
                         ).then_inc(s_p.sem, 1)
            on("tensor")(pe)

            def chunk(e, i, s, order):
                flat = agg[:, :, :].rearrange("p b d -> p (b d)")
                e.tensor_copy(flat[:, bass.ds((i * SLOTS + s) * GB * D, GB * D)].rearrange("p (b d) -> p b d", d=D),
                              G[s][:, 0:GB, 0:D]).then_inc(s_free[s].sem, 1)
                order(e.memset(sink[:, :], 0.0))
            chunk.steps = 1
            gather(name, ends_i, {"act": [(s_v, ends_ready)], "pool": [(s_tab, tab)]},
                   scanned, D, GB, GROUPS // SLOTS, chunk)

            def vec_fix(e):
                e.wait_ge(s_p.sem, p0 + 3)
                flat = agg[:, :, :].rearrange("p b d -> p (b d)")
                tflat = tmp[:, :, :].rearrange("p b d -> p (b d)")
                w = NB * D // 4
                if is_max:
                    step(e, e.tensor_scalar(stat[:, :], pY[0][:, 2, 0:NB], BIG, -BIG, ALU.mult, ALU.add))
                    for k in range(4):
                        ins = e.tensor_copy(tflat[:, k * w:(k + 1) * w], pY[k // 2][:, k % 2, 0:w])
                    step(e, ins)
                    step(e, tt(e, tmp[:, :, :], tmp[:, :, :], spread(stat[:, :]), ALU.add))
                    step(e, tt(e, agg[:, :, :], agg[:, :, :], tmp[:, :, :], ALU.max))
                else:
                    for k in range(4):
                        ins = tt(e, tflat[:, k * w:(k + 1) * w], flat[:, k * w:(k + 1) * w],
                                 pY[k // 2][:, k % 2, 0:w], ALU.add)
                    step(e, ins)
                    step(e, tt(e, agg[:, :, :], tmp[:, :, :], spread(has[:, :]), ALU.mult))
            on("vector")(vec_fix)

        def batch_norm(layer):
            p0, v0, a0 = s_p.n, s_v.n, s_a.n
            bump(s_p, 2)
            bump(s_v, 3)
            bump(s_a)
            per_feature = "p b d -> p d b"

            def pads_to_zero(e, t):
                step(e, e.tensor_scalar(t[:, NB - 1, :], t[:, NB - 1, :], real[:, 0:1], None, ALU.mult))

            def over_blocks(t):
                return t.unsqueeze(1).to_broadcast([P, NB, D])

            def vec(e):
                step(e, tt(e, agg[:, :, :], agg[:, :, :], root[:, :, :], ALU.add))
                pads_to_zero(e, agg)
                e.tensor_reduce(bn[:, 0, :], agg[:, :, :].rearrange(per_feature), AX.X, ALU.add
                                ).then_inc(s_v.sem, 1)
                e.wait_ge(s_p.sem, p0 + 1)
                step(e, e.tensor_scalar(bn[:, 1, :], pT[0][:, 0:D], 1.0 / N, None, ALU.mult))
                step(e, tt(e, agg[:, :, :], agg[:, :, :], over_blocks(bn[:, 1, :]), ALU.subtract))
                pads_to_zero(e, agg)
                step(e, tt(e, tmp[:, :, :], agg[:, :, :], agg[:, :, :], ALU.mult))
                e.tensor_reduce(bn[:, 0, :], tmp[:, :, :].rearrange(per_feature), AX.X, ALU.add
                                ).then_inc(s_v.sem, 1)
                e.wait_ge(s_p.sem, p0 + 2)
                e.tensor_scalar(bn[:, 1, :], pT[0][:, 0:D], 1.0 / N, BN_EPS, ALU.mult, ALU.add
                                ).then_inc(s_v.sem, 1)
                e.wait_ge(s_a.sem, a0 + 1)
                step(e, e.reciprocal(bn[:, 3, :], bn[:, 2, :]))
                step(e, tt(e, bn[:, 3, :], bn[:, 3, :], gamma[:, layer, :], ALU.mult))
                step(e, tt(e, tmp[:, :, :], agg[:, :, :], over_blocks(bn[:, 3, :]), ALU.mult))
                step(e, tt(e, tmp[:, :, :], tmp[:, :, :], over_blocks(beta[:, layer, :]), ALU.add))
                step(e, e.tensor_scalar(h[:, :, :], tmp[:, :, :], 0.0, None, ALU.max))
            on("vector")(vec)

            def pe(e):
                for k in range(2):
                    e.wait_ge(s_v.sem, v0 + 1 + k)
                    e.matmul(pT[0][:, 0:D], ones[:, :], bn[:, 0, :], start=True, stop=True
                             ).then_inc(s_p.sem, 1)
            on("tensor")(pe)

            def act(e):
                e.wait_ge(s_v.sem, v0 + 3)
                e.activation(bn[:, 2, :], bn[:, 1, :], ACT.Sqrt).then_inc(s_a.sem, 1)
            on("scalar")(act)
            publish_h()

        norm_relu()
        ends_ready = None
        for layer in range(LAYERS):
            if layer:
                mm = [c.n for c in s_mm]
                nxt = layer

                def load_w(e, mm=mm, nxt=nxt):
                    for s in range(SLOTS):
                        e.wait_ge(s_mm[s].sem, mm[s])
                    e.dma_start(conv_w[:, :], io["conv_w"][nxt]).then_inc(s_w.sem, 16)
                on("sync")(load_w)
                bump(s_w, 16)

            def conv_out(e, s, ps, g, k, m):
                e.tensor_copy(rows[s][:, k:k + m, :], ps[:, :, 0:ROW])
                flat = root[:, :, :].rearrange("p b d -> p (b d)")
                return e.tensor_copy(flat[:, bass.ds(g * (GB * D) + k * D, m * D)].rearrange(
                    "p (b d) -> p b d", d=D), ps[:, :, ROW:CW])
            node_product(conv_w, CW, conv_out, True,
                         (s_w, s_w.n) if layer else (s_in, IN_ALL))
            edges(f"conv{layer}", conv_table, ROW, io["attr"], EF, {"pool": [(s_tab, s_tab.n)],
                  "act": [(s_in, IN_ALL)]}, False, layer == 0)
            if layer == 0:
                ends_ready = node_ends()
            nodes(f"end{layer}", False, ends_ready)
            if layer < LAYERS - 1:
                batch_norm(layer)
            else:
                def last_relu(e):
                    step(e, tt(e, agg[:, :, :], agg[:, :, :], root[:, :, :], ALU.add))
                    step(e, e.tensor_scalar(h[:, :, :], agg[:, :, :], 0.0, None, ALU.max))
                on("vector")(last_relu)
                publish_h()

        def residual_out(e, s, ps, g, k, m):
            flat = x[:, :, :].rearrange("p b d -> p (b d)")
            there = flat[:, bass.ds(g * (GB * D), GB * D)]
            return e.tensor_tensor(there, there, ps.rearrange("p b c -> p (b c)"), ALU.add)

        node_product(lin_w[:, 0, :], D, residual_out, False)
        all_rows = [c.n for c in s_rows]

        def order_x(e):
            for s in range(SLOTS):
                e.wait_ge(s_rows[s].sem, all_rows[s])
        on("vector")(order_x)

        norm_relu()
        h_ready = s_v.n
        max_stored = sem("s_max_table")

        def store_h(e):
            e.wait_ge(s_v.sem, h_ready)
            e.dma_start(max_table.rearrange("(b p) c -> p b c", p=P), h[:, :, :]).then_inc(max_stored.sem, 16)
        on("sync")(store_h)

        def to_max(e):
            step(e, e.tensor_scalar(same[:, :], same[:, :], BIG, -BIG, ALU.mult, ALU.add))
        on("vector")(to_max)
        edges("max", max_table, D, io["weight"], 1, {"pool": [(max_stored, 16)]}, True, False)
        nodes("end_max", True, ends_ready)

        def take_agg(e):
            step(e, e.tensor_copy(h[:, :, :], agg[:, :, :]))
        on("vector")(take_agg)
        publish_h()
        node_product(lin_w[:, 1, :], D, residual_out, False)
        done = [c.n for c in s_rows]

        def write_out(e):
            for s in range(SLOTS):
                e.wait_ge(s_rows[s].sem, done[s])
            e.dma_start(io["out"], x[:, :, :]).then_inc(s_out.sem, 16)
            e.wait_ge(s_out.sem, 16)
        on("sync")(write_out)

        block = ctx.enter_context(nc.Block())

        def attach(decorate, name):
            @decorate
            def _(e):
                for f in programs[name]:
                    f(e)
        attach(block.sync, "sync")
        attach(block.gpsimd, "gpsimd")
        attach(block.scalar, "scalar")
        attach(block.vector, "vector")
        attach(block.tensor, "tensor")


def kernel(**inputs):
    import concourse.bacc as _bacc
    from concourse.bass_utils import run_bass_kernel_spmd as _run

    def streams(a, fill):
        a = np.asarray(a).reshape(E, -1)
        out = np.full((EPAD, a.shape[1]), fill, a.dtype)
        out[:E] = a
        return out.reshape(P, -1)

    def diagonal(blocks, width, bias):
        out = np.zeros((GB * D + 1, GB * width), np.float32)
        for b in range(GB):
            out[b * D:(b + 1) * D, b * width:(b + 1) * width] = blocks
            out[GB * D, b * width:(b + 1) * width] = bias
        return out

    f = {k: np.asarray(v) for k, v in inputs.items()}
    dst = streams(f["dst"], NPAD - 1)
    first, last = dst[:, 0], dst[:, -1]
    none = np.full(1, -1, dst.dtype)
    prev_last, prev_first = np.concatenate([none, last[:-1]]), np.concatenate([none, first[:-1]])
    next_first = np.concatenate([first[1:], none])

    x = np.zeros((NPAD, D), np.float32)
    x[:N] = f["x"]
    conv_w = []
    for layer in range(LAYERS):
        ew = f["L0_gnn_edge_w"][layer].reshape(EF, D, D).transpose(1, 0, 2).reshape(D, EF * D)
        eb = f["L0_gnn_edge_b"][layer].reshape(D, D)
        block = np.concatenate([ew, eb, f["L0_gnn_root_w"][layer]], axis=1)
        bias = np.concatenate([np.zeros(ROW, np.float32), f["L0_gnn_root_b"][layer]])
        conv_w.append(diagonal(block, CW, bias))
    lin_w = np.stack([diagonal(f["L0_gnn_pred_w"], D, f["L0_gnn_pred_b"]),
                      diagonal(f["L1_gnn_W"].T, D, f["L1_gnn_b"])], axis=1)
    order = np.arange(P)
    arrays = {
        "src": streams(f["src"], 0), "dst": dst, "attr": streams(f["edge_attr_8"], 0),
        "weight": streams(f["edge_weight1"], 0),
        "x": x.reshape(NB, P, D).transpose(1, 0, 2),
        "ident": np.eye(P, dtype=np.float32),
        "upper": (order[:, None] <= order[None, :]).astype(np.float32),
        "lanes": np.broadcast_to(order.astype(np.float32), (P, P)),
        "real": (order < LAST).astype(np.float32)[:, None],
        "lin_w": lin_w, "conv_w": np.stack(conv_w),
        "gamma": np.broadcast_to(f["L0_gnn_bn_gamma"], (P, LAYERS - 1, D)),
        "beta": np.broadcast_to(f["L0_gnn_bn_beta"], (P, LAYERS - 1, D)),
        "borders": np.stack([first, last, prev_last, next_first], axis=1),
        "borders_row": np.broadcast_to(np.stack([first, prev_last, prev_first]), (D, 3, P)),
    }
    nc = _bacc.Bacc("TRN2", target_bir_lowering=False, num_devices=1)
    arrays = {f"in_{k}": np.ascontiguousarray(v) for k, v in arrays.items()}
    io = {k[3:]: nc.dram_tensor(k, v.shape, mybir.dt.from_np(v.dtype), kind="ExternalInput").ap()
          for k, v in arrays.items()}
    io["out"] = nc.dram_tensor("out", (P, NB, D), F32, kind="ExternalOutput").ap()
    build(nc, io)
    got = _run(nc, [arrays], core_ids=[0]).results[0]["out"]
    return np.asarray(got).transpose(1, 0, 2).reshape(NPAD, D)[:N]
```

```python
import numpy as np
import concourse.bass as bass
from concourse import mybir
from contextlib import ExitStack

F32, BF16, F16, I32 = mybir.dt.float32, mybir.dt.bfloat16, mybir.dt.float16, mybir.dt.int32
ALU = mybir.AluOpType
ACT = mybir.ActivationFunctionType
AX = mybir.AxisListType

P = 128
N, D, EF, E, LAYERS = 12500, 16, 8, 412500, 3
FB = EF + 1
ROW = FB * D
NB = -(-N // P)
NPAD = NB * P
LAST = N - (NB - 1) * P
T = 26
CHUNKS = 124
STREAM = T * CHUNKS
EPAD = P * STREAM
SLOTS = 2
GB = 7
GROUPS = NB // GB
CW = ROW + D
PER_BANK = 512 // CW
TP = 7
TG = T - TP
QUARTERS = 4
FARS = -(-NB // QUARTERS)
PE_EDGES = TP * P
FAR = 2.0 ** 126
BIG = 1.5e38
LN_EPS = BN_EPS = 1e-5
assert EPAD >= E and E > (P - 1) * STREAM and GROUPS * GB == NB and GROUPS % SLOTS == 0
assert CHUNKS % SLOTS == 0 and CHUNKS <= P and TP == GB and FARS * D <= 512


class Count:
    def __init__(self, sem):
        self.sem, self.n = sem, 0


def build(nc, io):
    ctx = ExitStack()

    def sb(name, shape, dt=F32):
        return ctx.enter_context(nc.sbuf_tensor(name, shape, dt))

    def sem(name):
        return Count(ctx.enter_context(nc.semaphore(name)))

    def slots(make, name, *a):
        return [make(f"{name}{s}", *a) for s in range(SLOTS)]

    with ctx:
        conv_table = nc.dram_tensor("conv_table", (NPAD, ROW), F32, kind="Internal").ap()
        max_table = nc.dram_tensor("max_table", (NPAD, D), F32, kind="Internal").ap()
        scanned = nc.dram_tensor("scanned", (EPAD, D), F32, kind="Internal").ap()
        key_rows = nc.dram_tensor("key_rows", (CHUNKS, PE_EDGES), F16, kind="Internal").ap()
        far_rows = nc.dram_tensor("far_rows", (CHUNKS, PE_EDGES), F16, kind="Internal").ap()
        conv_rows = conv_table.rearrange("(b p) c -> p b c", p=P)
        scanned_rows = scanned.rearrange("(p t) c -> p (t c)", p=P)

        src = sb("src", [P, STREAM], I32)
        dst = sb("dst", [P, STREAM], I32)
        same = sb("same", [P, STREAM])
        x = sb("x_res", [P, NB, D])
        h = sb("h", [P, NB, D])
        agg = sb("agg", [P, NB, D])
        root = sb("root", [P, NB, D])
        tmp = sb("tmp", [P, NB, D])
        ident = sb("ident", [P, P])
        upper = sb("upper", [P, P])
        ones = sb("ones", [P, P])
        lanes = sb("lanes", [P, P])
        lanes_b = sb("lanes_b", [P, P], BF16)
        real = sb("real", [P, 1])
        conv_w = sb("conv_w", [GB * D + 1, GB * CW])
        lin_w = sb("lin_w", [GB * D + 1, 2, GB * D])
        gamma = sb("gamma", [P, LAYERS - 1, D])
        beta = sb("beta", [P, LAYERS - 1, D])
        ends_i = sb("ends_i", [P, NB], I32)
        has = sb("has", [P, NB])
        cnt = sb("cnt", [P, NB])
        cum = sb("cum", [P, NB])
        tot = sb("tot", [P, NB])
        stat = sb("stat", [P, NB])
        stat2 = sb("stat2", [P, NB])
        bn = sb("bn", [P, 4, D])
        sink = sb("sink", [P, 1])
        zeros = sb("zeros", [P, P], BF16)
        edge_i = sb("edge_i", [P, 4], I32)
        edge_m = sb("edge_m", [P, 6])
        head_lo = sb("head_lo", [P, P])
        head_hi = sb("head_hi", [P, NB])
        head_lo_i = sb("head_lo_i", [P, 2], I32)
        row_i = sb("row_i", [D, 3, P], I32)
        row_m = sb("row_m", [D, 6, P])
        state = sb("state", [P, D])
        state_row = sb("state_row", [D, P])
        carry_row = sb("carry_row", [D, P])
        carry = sb("carry", [P, D + 1])
        carry_hi = sb("carry_hi", [P, NB, D])

        idx = slots(sb, "idx", [P, T], I32)
        G = slots(sb, "gathered", [P, T, ROW])
        attr = slots(sb, "attr", [P, T, EF])
        msg = sb("msg", [P, T, D])
        run = slots(sb, "run", [P, T, D])
        dst_i = slots(sb, "dst_i", [P, 2, T], I32)
        dst_b = slots(sb, "dst_b", [P, 2, T], BF16)
        hot_lo = slots(sb, "hot_lo", [P, T, P], BF16)
        hot_hi = slots(sb, "hot_hi", [P, T, NB], BF16)
        parts = [sb(f"part{k}", [P, FARS * QUARTERS, D], BF16) for k in range(3)]
        quarter_lane = sb("quarter_lane", [P, QUARTERS])
        far_mask = sb("far_mask", [FARS, FARS, D], BF16)
        keys = slots(sb, "keys", [P, PE_EDGES], F16)
        fars = slots(sb, "fars", [FARS, PE_EDGES], F16)
        hot_key = slots(sb, "hot_key", [P, QUARTERS, PE_EDGES], BF16)
        not_far = slots(sb, "not_far", [FARS, PE_EDGES], BF16)
        xe = slots(sb, "xe", [P, TP * D])
        xeT = sb("xeT", [TP * D, P])
        pe_src = sb("pe_src", [CHUNKS, PE_EDGES], I32)
        pe_tmp = sb("pe_tmp", [CHUNKS, PE_EDGES], I32)
        hs = slots(sb, "hs", [P, GB * D + 1])
        hT = slots(sb, "hT", [GB * D + 1, P])
        rows = slots(sb, "rows", [P, GB, ROW])

        pT = [ctx.enter_context(nc.psum_tensor(f"pT{s}", [P, 512], F32)) for s in range(SLOTS)]
        pY = [ctx.enter_context(nc.psum_tensor(f"pY{s}", [P, 3, 512], F32)) for s in range(SLOTS)]
        pC = pT[1]
        pE = pY[0]
        pG = [pY[1][:, k, 0:FARS * D] for k in range(2)]

        s_in = sem("s_in")
        s_w = sem("s_w")
        s_init = sem("s_init")
        s_free = slots(sem, "s_free")
        s_idx = slots(sem, "s_idx")
        s_run = slots(sem, "s_run")
        s_runfree = slots(sem, "s_runfree")
        s_step = sem("s_step")
        s_hot = slots(sem, "s_hot")
        s_hotfree = slots(sem, "s_hotfree")
        s_hs = slots(sem, "s_hs")
        s_tr = slots(sem, "s_tr")
        s_hT = slots(sem, "s_hT")
        s_mm = slots(sem, "s_mm")
        s_rows = slots(sem, "s_rows")
        s_rowsfree = slots(sem, "s_rowsfree")
        s_keys = sem("s_keys")
        s_hotk = slots(sem, "s_hotk")
        s_gath = sem("s_gath")
        s_pick = sem("s_pick")
        s_xt = sem("s_xt")
        s_xeT = sem("s_xeT")
        s_prod = sem("s_prod")
        s_rowsG = slots(sem, "s_rowsG")
        s_v = sem("s_v")
        s_p = sem("s_p")
        s_a = sem("s_a")
        s_tab = sem("s_tab")
        s_out = sem("s_out")
        tick = {e: sem(f"s_tick_{e}") for e in ("pool", "act", "dve", "pe", "sp")}

        programs = {e: [] for e in ("sync", "gpsimd", "scalar", "vector", "tensor")}

        def on(engine):
            return programs[engine].append

        def gate(eng, who, s, value):
            eng.wait_ge(s.sem, value)
            eng.sem_inc(tick[who].sem, 1)

        def bump(s, n=1):
            s.n += n
            return s.n

        loads = [(src, io["src"]), (dst, io["dst"]), (x, io["x"]), (ident, io["ident"]),
                 (upper, io["upper"]), (lanes, io["lanes"]), (real, io["real"]),
                 (lin_w, io["lin_w"]), (gamma, io["gamma"]), (beta, io["beta"]),
                 (edge_i, io["borders"]), (pe_src, io["pe_src"]),
                 (quarter_lane, io["quarter_lane"]), (far_mask, io["far_mask"]), (row_i, io["borders_row"]), (conv_w, io["conv_w"][0])]

        def sync_start(e):
            for tile, ap in loads:
                shape = list(tile.shape)
                e.dma_start(tile[tuple(slice(None) for _ in shape)], ap).then_inc(s_in.sem, 16)
        on("sync")(sync_start)
        bump(s_in, 16 * len(loads))
        IN_ALL = s_in.n

        def step(e, ins):
            ins.then_inc(s_step.sem, 1)
            s_step.n += 1
            e.wait_ge(s_step.sem, s_step.n)

        def tt(e, out, a, b, op):
            return e.tensor_tensor(out, a, b, op)

        INIT_ALL = 3 + 2 * SLOTS

        def vector_start(e):
            e.memset(ones[:, :], 1.0).then_inc(s_init.sem, 1)
            e.memset(zeros[:, :], 0.0).then_inc(s_init.sem, 1)
            for s in range(SLOTS):
                e.memset(hs[s][:, :], 1.0).then_inc(s_init.sem, 1)
                e.memset(run[s][:, :, :], 0.0).then_inc(s_init.sem, 1)
                e.memset(G[s][:, 0, 0:1], 0.0).then_inc(s_free[s].sem, 1)
            e.memset(carry[:, D:D + 1], 1.0).then_inc(s_init.sem, 1)
            e.wait_ge(s_in.sem, IN_ALL)
            e.wait_ge(s_init.sem, INIT_ALL)
            step(e, e.memset(same[:, 0:1], 0.0))
            e.tensor_tensor(same[:, 1:STREAM], dst[:, 1:STREAM], dst[:, 0:STREAM - 1], ALU.is_equal)
            first, last, prev_last, next_first = (edge_i[:, k:k + 1] for k in range(4))
            tt(e, edge_m[:, 0:1], first, prev_last, ALU.is_equal)
            tt(e, edge_m[:, 1:2], first, last, ALU.is_equal)
            step(e, tt(e, edge_m[:, 2:3], next_first, last, ALU.is_equal))
            step(e, tt(e, edge_m[:, 3:4], edge_m[:, 1:2], edge_m[:, 2:3], ALU.mult))
            step(e, e.tensor_scalar(edge_m[:, 4:5], edge_m[:, 3:4], -1.0, 1.0, ALU.mult, ALU.add))
            e.tensor_scalar(head_lo_i[:, 0:1], first, P - 1, None, ALU.bitwise_and)
            step(e, e.tensor_scalar(head_lo_i[:, 1:2], first, 7, None, ALU.logical_shift_right))
            step(e, e.tensor_copy(edge_m[:, 0:2], head_lo_i[:, 0:2]))
            step(e, e.tensor_scalar(head_lo[:, :], lanes[:, :], edge_m[:, 0:1], edge_m[:, 4:5],
                                    ALU.is_equal, ALU.mult))
            step(e, e.tensor_scalar(head_hi[:, :], lanes[:, 0:NB], edge_m[:, 1:2], None, ALU.is_equal))
            rf, rpl, rpf = (row_i[:, k, :] for k in range(3))
            tt(e, row_m[:, 0, :], rf, rpl, ALU.is_equal)
            step(e, tt(e, row_m[:, 1, :], rpf, rpl, ALU.is_equal))
            step(e, tt(e, row_m[:, 2, :], row_m[:, 0, :], row_m[:, 1, :], ALU.mult))
            e.tensor_scalar(row_m[:, 3, :], row_m[:, 0, :], BIG, -BIG, ALU.mult, ALU.add)
            step(e, e.tensor_scalar(row_m[:, 4, :], row_m[:, 2, :], BIG, -BIG, ALU.mult, ALU.add))
            e.tensor_copy(lanes_b[:, :], lanes[:, :])
            for part in parts:
                e.memset(part[:, NB:FARS * QUARTERS, :], 0.0)
            step(e, e.tensor_scalar(pe_tmp[:, :], pe_src[:, :], QUARTERS * P - 1, None, ALU.bitwise_and))
            step(e, e.tensor_copy(keys[0][0:CHUNKS, :], pe_tmp[:, :]))
            step(e, e.tensor_scalar(pe_tmp[:, :], pe_src[:, :], 9, None, ALU.logical_shift_right))
            e.tensor_copy(keys[1][0:CHUNKS, :], pe_tmp[:, :]).then_inc(s_v.sem, 1)
        on("vector")(vector_start)
        bump(s_v)

        def sync_keys(e):
            e.wait_ge(s_v.sem, 1)
            for ap, half in ((key_rows, keys[0]), (far_rows, keys[1])):
                e.dma_start(ap, half[0:CHUNKS, :]).then_inc(s_keys.sem, 16)
            e.wait_ge(s_keys.sem, 32)
        on("sync")(sync_keys)
        assert QUARTERS * P == 1 << 9

        def credits(name, engine, counts):
            def f(e):
                for c in counts:
                    e.sem_inc(c.sem, 1)
            on(engine)(f)
            for c in counts:
                c.n = 1
        for c in s_free:
            c.n = 1
        credits("sp", "sync", s_runfree + s_rowsfree)
        credits("pe", "tensor", s_tr + s_mm + s_hotfree + [s_prod])
        credits("act", "scalar", s_rowsG)
        credits("dve", "vector", [s_pick, s_pick])
        s_pick.n = 2
        credits("dve", "vector", s_rows)
        for c in s_rows:
            c.n = 1

        def spread(t):
            return t.unsqueeze(2).to_broadcast([P, NB, D])

        def norm_relu():
            a0 = s_a.n
            bump(s_a)
            bump(s_v)
            v0 = s_v.n

            def vec(e):
                step(e, e.tensor_reduce(stat[:, :], x[:, :, :], AX.X, ALU.add))
                step(e, e.tensor_scalar(stat[:, :], stat[:, :], 1.0 / D, None, ALU.mult))
                step(e, tt(e, h[:, :, :], x[:, :, :], spread(stat[:, :]), ALU.subtract))
                step(e, tt(e, tmp[:, :, :], h[:, :, :], h[:, :, :], ALU.mult))
                step(e, e.tensor_reduce(stat2[:, :], tmp[:, :, :], AX.X, ALU.add))
                e.tensor_scalar(stat2[:, :], stat2[:, :], 1.0 / D, LN_EPS, ALU.mult,
                                ALU.add).then_inc(s_v.sem, 1)
                e.wait_ge(s_a.sem, a0 + 1)
                step(e, e.reciprocal(stat2[:, :], stat[:, :]))
                step(e, tt(e, tmp[:, :, :], h[:, :, :], spread(stat2[:, :]), ALU.mult))
                step(e, e.tensor_scalar(h[:, :, :], tmp[:, :, :], 0.0, None, ALU.max))
            on("vector")(vec)

            def act(e):
                e.wait_ge(s_v.sem, v0)
                e.activation(stat[:, :], stat2[:, :], ACT.Sqrt).then_inc(s_a.sem, 1)
            on("scalar")(act)
            publish_h()

        def publish_h():
            bump(s_v)
            on("vector")(lambda e: e.memset(sink[:, :], 0.0).then_inc(s_v.sem, 1))

        def node_product(weights, width, out_fn, store, wait_weights=None):
            v_ready = s_v.n
            b = {k: [c.n for c in cs] for k, cs in
                 dict(hs=s_hs, tr=s_tr, hT=s_hT, mm=s_mm, rows=s_rows, rf=s_rowsfree).items()}
            per_bank = 512 // width if width * GB > 512 else GB
            pieces = [(k, min(per_bank, GB - k)) for k in range(0, GB, per_bank)]
            store_sems = slots(sem, f"s_store{len(programs['sync'])}_") if store else None

            def act(e):
                e.wait_ge(s_v.sem, v_ready)
                with e.Fori(0, GROUPS // SLOTS) as i:
                    for s in range(SLOTS):
                        gate(e, "act", s_tr[s], i + b["tr"][s])
                        hf = h[:, :, :].rearrange("p b d -> p (b d)")
                        e.copy(hs[s][:, 0:GB * D],
                               hf[:, bass.ds((i * SLOTS + s) * GB * D, GB * D)]).then_inc(s_hs[s].sem, 1)
                    for s in range(SLOTS):
                        gate(e, "act", s_tr[s], i + b["tr"][s] + 1)
                        gate(e, "act", s_mm[s], i + b["mm"][s])
                        e.copy(hT[s][:, :], pT[s][0:GB * D + 1, 0:P]).then_inc(s_hT[s].sem, 1)
            on("scalar")(act)

            def pe(e):
                if wait_weights is not None:
                    e.wait_ge(wait_weights[0].sem, wait_weights[1])
                with e.Fori(0, GROUPS // SLOTS) as i:
                    for s in range(SLOTS):
                        gate(e, "pe", s_hs[s], i + b["hs"][s] + 1)
                        e.transpose(pT[s][0:GB * D + 1, 0:P], hs[s][:, :], ident[:, :]).then_inc(s_tr[s].sem, 1)
                    for s in range(SLOTS):
                        gate(e, "pe", s_hT[s], i + b["hT"][s] + 1)
                        gate(e, "pe", s_rows[s], i + b["rows"][s])
                        for n, (k, m) in enumerate(pieces):
                            ins = e.matmul(pY[s][:, n, 0:m * width], hT[s][:, :],
                                           weights[:, k * width:(k + m) * width], start=True, stop=True)
                        ins.then_inc(s_mm[s].sem, 1)
            on("tensor")(pe)

            def vec(e):
                with e.Fori(0, GROUPS // SLOTS) as i:
                    for s in range(SLOTS):
                        gate(e, "dve", s_mm[s], i + b["mm"][s] + 1)
                        if store:
                            gate(e, "dve", s_rowsfree[s], i + b["rf"][s])
                        for n, (k, m) in enumerate(pieces):
                            ps = pY[s][:, n, 0:m * width].rearrange("p (b c) -> p b c", c=width)
                            ins = out_fn(e, s, ps, i * SLOTS + s, k, m)
                        ins.then_inc(s_rows[s].sem, 1)
            on("vector")(vec)

            it = GROUPS // SLOTS
            if store:
                def sp(e):
                    with e.Fori(0, it) as i:
                        for s in range(SLOTS):
                            gate(e, "sp", s_rows[s], i + b["rows"][s] + 1)
                            e.dma_start(conv_rows[:, bass.ds((i * SLOTS + s) * GB, GB), :],
                                        rows[s][:, :, :]).then_inc(store_sems[s].sem, 16)
                        for s in range(SLOTS):
                            gate(e, "sp", store_sems[s], i * 16 + 16)
                            e.sem_inc(s_rowsfree[s].sem, 1)
                    e.sem_inc(s_tab.sem, 1)
                on("sync")(sp)
                bump(s_tab)
            for cs in (s_hs, s_tr, s_hT, s_mm, s_rows) + ((s_rowsfree,) if store else ()):
                for c in cs:
                    bump(c, it)

        def gather(name, indices, ready, table, width, steps, stride, iters, vec_chunk=None, act_after=None):
            got = slots(sem, f"s_got_{name}")
            b_free, b_idx = [c.n for c in s_free], [c.n for c in s_idx]

            def act(e):
                for c, v in ready.get("act", ()):
                    e.wait_ge(c.sem, v)
                with e.Fori(0, iters) as i:
                    for s in range(SLOTS):
                        gate(e, "act", s_free[s], i + b_free[s])
                        e.copy(idx[s][:, 0:steps], indices[:, bass.ds((i * SLOTS + s) * stride, steps)]
                               ).then_inc(s_idx[s].sem, 1)
                        if act_after is not None:
                            act_after(e, i, s)
            on("scalar")(act)

            def pool(e):
                for c, v in ready.get("pool", ()):
                    e.wait_ge(c.sem, v)
                with e.Fori(0, iters) as i:
                    for s in range(SLOTS):
                        gate(e, "pool", s_idx[s], i + b_idx[s] + 1)
                        for t in range(steps):
                            e.indirect_dma_start(
                                out=G[s][:, t, 0:width], out_offset=None, in_=table[:, :],
                                in_offset=bass.IndirectOffsetOnAxis(ap=idx[s][:, t:t + 1], axis=0)
                            ).then_inc(got[s].sem, 16)
            on("gpsimd")(pool)

            if vec_chunk is not None:
                def vec(e):
                    with e.Fori(0, iters) as i:
                        for s in range(SLOTS):
                            gate(e, "dve", got[s], (i + 1) * (16 * steps))
                            vec_chunk(e, i, s)
                on("vector")(vec)
            for c in s_free + s_idx:
                bump(c, iters)
            return got

        def edges(name, table, width, attr_dram, attr_width, ready, is_max, count, v_parts):
            iters = CHUNKS // SLOTS
            b_free, b_run, b_rf, b_hot, b_hf, b_hotk, b_rg = (
                [c.n for c in cs] for cs in (s_free, s_run, s_runfree, s_hot, s_hotfree, s_hotk, s_rowsG))
            b_gath, b_pick, b_xt, b_xeT, b_prod = (c.n for c in (s_gath, s_pick, s_xt, s_xeT, s_prod))
            loaded = slots(sem, f"s_attr_{name}")
            keyed = slots(sem, f"s_keyed_{name}")
            stored = slots(sem, f"s_stored_{name}")
            HEAD = 3

            def load_keys(e, n, s):
                e.dma_start(keys[s][:, :], key_rows[bass.ds(n, 1), :].to_broadcast([P, PE_EDGES])
                            ).then_inc(keyed[s].sem, 16)
                e.dma_start(fars[s][:, :], far_rows[bass.ds(n, 1), :].to_broadcast([FARS, PE_EDGES])
                            ).then_inc(keyed[s].sem, 16)

            def sp_pair(e, i, more_keys):
                for s in range(SLOTS):
                    gate(e, "sp", s_free[s], i + b_free[s])
                    e.dma_start(attr[s][:, :, 0:attr_width].rearrange("p t f -> p (t f)")
                                if attr_width == EF else attr1[s],
                                attr_dram[:, bass.ds((i * SLOTS + s) * T * attr_width, T * attr_width)]
                                ).then_inc(loaded[s].sem, 16)
                    if more_keys:
                        gate(e, "sp", s_hotk[s], i + b_hotk[s] + 1)
                        load_keys(e, i * SLOTS + s + SLOTS, s)
                for s in range(SLOTS):
                    gate(e, "sp", s_run[s], i + b_run[s] + 1)
                    e.dma_start(scanned_rows[:, bass.ds((i * SLOTS + s) * T * D, T * D)],
                                run[s][:, :, :].rearrange("p t d -> p (t d)")).then_inc(stored[s].sem, 16)
                for s in range(SLOTS):
                    gate(e, "sp", stored[s], i * 16 + 16)
                    e.sem_inc(s_runfree[s].sem, 1)

            def sp(e):
                for s in range(SLOTS):
                    if b_hotk[s]:
                        e.wait_ge(s_hotk[s].sem, b_hotk[s])
                    load_keys(e, s, s)
                with e.Fori(0, iters - 1) as i:
                    sp_pair(e, i, True)
                sp_pair(e, iters - 1, False)
                e.sem_inc(s_tab.sem, 1)
            on("sync")(sp)
            bump(s_tab)

            def after(i, s):
                return (i, 1) if s == 0 else (i + 1, 0)

            def pe_step(e, i, s, j):
                g = s * TP + j
                bank = g % 2
                gate(e, "pe", s_pick, i * (SLOTS * TP) + (b_pick + g - 1))
                for q in range(QUARTERS):
                    for k, part in enumerate(parts):
                        view = part[:, :, :].rearrange("p (r q) d -> p q r d", q=QUARTERS)[:, q]
                        e.matmul(pG[bank], hot_key[s][:, q, j * P:(j + 1) * P], view,
                                 start=(q == 0 and k == 0), stop=False)
                e.matmul(pG[bank], not_far[s][:, j * P:(j + 1) * P], far_mask[:, :, :],
                         start=False, stop=True).then_inc(s_gath.sem, 1)

            def pe_body(e, i, s, more, counted):
                o = 1 - s
                ni, ns = after(i, s)
                n = i * SLOTS + s
                for j in range(HEAD, TP):
                    pe_step(e, i, s, j)
                if more:
                    gate(e, "pe", s_hotk[ns], ni + (b_hotk[ns] + 1))
                    pe_step(e, ni, ns, 0)
                if not is_max:
                    gate(e, "pe", s_pick, n * TP + (TP + b_pick))
                    e.transpose(pT[0][0:TP * D, 0:P], xe[s][:, :], ident[:, :]).then_inc(s_xt.sem, 1)
                if more:
                    pe_step(e, ni, ns, 1)
                if not is_max:
                    gate(e, "pe", s_xeT, n + (1 + b_xeT))
                    gate(e, "pe", s_rowsG[o], i + (b_rg[o] + s))
                    wv = conv_w[0:TP * D, :].rearrange("p (b c) -> p b c", c=CW)
                    for k, m in PE_PIECES:
                        ins = e.matmul(pE[:, k // PER_BANK, 0:m * ROW], xeT[:, :], wv[:, k:k + m, 0:ROW],
                                       start=True, stop=True)
                    ins.then_inc(s_prod.sem, 1)
                if counted:
                    pe_count(e, i - 1, s)
                if more:
                    pe_step(e, ni, ns, 2)

            def pe_count(e, i, s):
                gate(e, "pe", s_hot[s], i + (b_hot[s] + 1))
                for t in range(T):
                    ins = e.matmul(pC[:, 0:NB], hot_lo[s][:, t, :], hot_hi[s][:, t, :],
                                   start=False, stop=False, skip_group_check=True)
                ins.then_inc(s_hotfree[s].sem, 1)

            rows_taken = [c.n for c in s_rows]

            def pe(e):
                e.wait_ge(s_v.sem, v_parts)
                for s in range(SLOTS):
                    e.wait_ge(s_rows[s].sem, rows_taken[s])
                if count:
                    e.wait_ge(s_init.sem, INIT_ALL)
                    e.matmul(pC[:, 0:NB], zeros[:, :], zeros[:, 0:NB], start=True, stop=False,
                             skip_group_check=True).then_inc(s_p.sem, 1)
                e.wait_ge(s_hotk[0].sem, b_hotk[0] + 1)
                for j in range(HEAD):
                    pe_step(e, 0, 0, j)
                for s in range(SLOTS):
                    pe_body(e, 0, s, True, False)
                with e.Fori(1, iters - 1) as i:
                    for s in range(SLOTS):
                        pe_body(e, i, s, True, count)
                for s in range(SLOTS):
                    pe_body(e, iters - 1, s, s == 0, count)
                if count:
                    for s in range(SLOTS):
                        pe_count(e, iters - 1, s)
            on("tensor")(pe)
            if count:
                bump(s_p)
                for cc in s_hot + s_hotfree:
                    bump(cc, iters)

            def act_rows(e, i, s):
                n = i * SLOTS + s
                if is_max:
                    gate(e, "act", s_pick, n * TP + (TP + b_pick))
                    e.copy(G[s][:, TG:T, 0:D], xe[s][:, :].rearrange("p (t d) -> p t d", d=D)
                           ).then_inc(s_rowsG[s].sem, 1)
                    return
                gate(e, "act", s_xt, n + (1 + b_xt))
                gate(e, "act", s_prod, n + b_prod)
                e.copy(xeT[:, :], pT[0][0:TP * D, 0:P]).then_inc(s_xeT.sem, 1)
                gate(e, "act", s_prod, n + (1 + b_prod))
                for k, m in PE_PIECES:
                    ins = e.copy(G[s][:, TG + k:TG + k + m, :],
                                 pE[:, k // PER_BANK, 0:m * ROW].rearrange("p (t c) -> p t c", c=ROW))
                ins.then_inc(s_rowsG[s].sem, 1)

            def hots(e, i, s):
                gate(e, "dve", keyed[s], i * 32 + 32)
                for q in range(QUARTERS):
                    e.tensor_scalar(hot_key[s][:, q, :], keys[s][:, :], quarter_lane[:, q:q + 1], None,
                                    ALU.is_equal)
                e.tensor_scalar(not_far[s][:, :], fars[s][:, :], quarter_lane[0:FARS, 0:1], -FAR,
                                ALU.not_equal, ALU.mult).then_inc(s_hotk[s].sem, 1)

            def pick(e, i, s, j):
                g = s * TP + j
                gate(e, "dve", s_gath, i * (SLOTS * TP) + (b_gath + g + 1))
                e.tensor_reduce(xe[s][:, j * D:(j + 1) * D], pG[g % 2].rearrange("p (r d) -> p d r", d=D),
                                AX.X, ALU.max).then_inc(s_pick.sem, 1)

            MARKS = (1 if is_max else 3) + (2 if count else 0)
            base = [0]

            def body(e, i, s, hot, pick_next, pick_head, got):
                n = i * SLOTS + s
                ni, ns = after(i, s)
                marks = [0]

                def mark(ins):
                    ins.then_inc(s_step.sem, 1)
                    marks[0] += 1
                    return marks[0]

                def need(k):
                    gate(e, "dve", s_step, n * MARKS + (base[0] + k))

                def pick_rest(j):
                    if pick_next:
                        pick(e, ni, ns, j)

                def pick_first(j):
                    if pick_head:
                        pick(e, i + 1, s, j)

                if hot:
                    hots(e, i + 1, s)
                pick_rest(3)
                gate(e, "dve", got[s], i * (16 * TG) + 16 * TG)
                gate(e, "dve", loaded[s], i * 16 + 16)
                g = G[s]
                if is_max:
                    pick_rest(4)
                    gate(e, "dve", s_rowsG[s], i + (b_rg[s] + 1))
                    m_all = mark(tt(e, msg[:, :, :], g[:, :, 0:D],
                                    attr1[s].unsqueeze(2).to_broadcast([P, T, D]), ALU.mult))
                    pick_rest(5)
                    need(m_all)
                    e.sem_inc(s_free[s].sem, 1)
                    pick_rest(6)
                else:
                    def product(a, b):
                        g4 = g[:, a:b, 0:EF * D].rearrange("p t (f d) -> p t f d", d=D)
                        return mark(tt(e, g4, g4, attr[s][:, a:b, :].unsqueeze(3).to_broadcast(
                            [P, b - a, EF, D]), ALU.mult))

                    def total(a, b):
                        return e.tensor_reduce(msg[:, a:b, :], g[:, a:b, :].rearrange(
                            "p t (f d) -> p t d f", d=D), AX.X, ALU.add)
                    half = T // 2
                    m_a = product(0, half)
                    pick_rest(4)
                    gate(e, "dve", s_rowsG[s], i + (b_rg[s] + 1))
                    m_b = product(half, T)
                    pick_rest(5)
                    need(m_a)
                    total(0, half)
                    pick_rest(6)
                    need(m_b)
                    m_all = mark(total(half, T))
                    pick_first(0)
                    need(m_all)
                    e.sem_inc(s_free[s].sem, 1)
                gate(e, "dve", s_runfree[s], i + b_rf[s])
                flags = same[:, bass.ds(n * T, T)]
                for d in range(D):
                    ins = e.tensor_tensor_scan(run[s][:, :, d], flags, msg[:, :, d],
                                               run[1 - s][:, T - 1, d:d + 1],
                                               ALU.add if is_max else ALU.mult,
                                               ALU.max if is_max else ALU.add)
                    if d == D - 1:
                        ins.then_inc(s_run[s].sem, 1)
                    if d == D // 2 and not is_max:
                        pick_first(1)
                if is_max:
                    pick_first(0)
                    pick_first(1)
                pick_first(2)
                if count:
                    gate(e, "dve", s_hotfree[s], i + b_hf[s])
                    dchunk = dst[:, bass.ds(n * T, T)]
                    e.tensor_scalar(dst_i[s][:, 0, :], dchunk, P - 1, None, ALU.bitwise_and)
                    need(mark(e.tensor_scalar(dst_i[s][:, 1, :], dchunk, 7, None, ALU.logical_shift_right)))
                    need(mark(e.tensor_copy(dst_b[s][:, :, :], dst_i[s][:, :, :])))
                    for k, hot_t, w in ((0, hot_lo[s], P), (1, hot_hi[s], NB)):
                        ins = tt(e, hot_t[:, :, :], dst_b[s][:, k, :].unsqueeze(2).to_broadcast([P, T, w]),
                                 lanes_b[:, 0:w].unsqueeze(1).to_broadcast([P, T, w]), ALU.is_equal)
                    ins.then_inc(s_hot[s].sem, 1)
                gate(e, "dve", s_run[s], i + (b_run[s] + 1))
                assert marks[0] == MARKS

            got = gather(name, src, ready, table, width, TG, T, iters, None, act_rows)

            def vec(e):
                base[0] = s_step.n
                for s in range(SLOTS):
                    hots(e, 0, s)
                for j in range(TP):
                    pick(e, 0, 0, j)
                for j in range(HEAD):
                    pick(e, 0, 1, j)
                with e.Fori(0, iters - 1) as i:
                    for s in range(SLOTS):
                        body(e, i, s, True, True, True, got)
                body(e, iters - 1, 0, False, True, False, got)
                body(e, iters - 1, 1, False, False, False, got)
                s_step.n += MARKS * CHUNKS
            on("vector")(vec)
            for cc in s_run + s_runfree + s_hotk + s_rowsG:
                bump(cc, iters)
            for cc in (s_gath, s_pick):
                bump(cc, CHUNKS * TP)
            if not is_max:
                for cc in (s_xt, s_xeT, s_prod):
                    bump(cc, CHUNKS)

        PE_PIECES = [(k, min(PER_BANK, TP - k)) for k in range(0, TP, PER_BANK)]

        def parts_of_h():
            v = bump(s_v)

            def vec(e):
                step(e, e.tensor_copy(parts[0][:, 0:NB, :], h[:, :, :]))
                step(e, tt(e, tmp[:, :, :], h[:, :, :], parts[0][:, 0:NB, :], ALU.subtract))
                step(e, e.tensor_copy(parts[1][:, 0:NB, :], tmp[:, :, :]))
                step(e, tt(e, tmp[:, :, :], tmp[:, :, :], parts[1][:, 0:NB, :], ALU.subtract))
                e.tensor_copy(parts[2][:, 0:NB, :], tmp[:, :, :]).then_inc(s_v.sem, 1)
            on("vector")(vec)
            return v

        attr1 = [a[:, :, :].rearrange("p t f -> p (t f)")[:, 0:T] for a in attr]

        def hand_over_vec():
            v = bump(s_v)
            on("vector")(lambda e: e.memset(sink[:, :], 0.0).then_inc(s_v.sem, 1))
            return v

        def node_ends():
            p0, v0 = s_p.n, s_v.n
            hf = [c.n for c in s_hotfree]
            bump(s_p)
            bump(s_v, 2)

            def vec1(e):
                for s in range(SLOTS):
                    e.wait_ge(s_hotfree[s].sem, hf[s])
                e.tensor_copy(cnt[:, :], pC[:, 0:NB]).then_inc(s_v.sem, 1)
                e.wait_ge(s_p.sem, p0 + 1)
                step(e, e.tensor_copy(tot[:, :], pC[:, NB:2 * NB]))
                step(e, e.tensor_tensor_scan(cum[:, :], tot[:, :], tot[:, :], 0.0, ALU.add, ALU.max))
                step(e, tt(e, cum[:, :], cum[:, :], tot[:, :], ALU.subtract))
                step(e, tt(e, cum[:, :], cum[:, :], pC[:, 2 * NB:3 * NB], ALU.add))
                e.tensor_scalar(has[:, :], cnt[:, :], 1.0, None, ALU.min)
                step(e, e.tensor_scalar(cum[:, :], cum[:, :], -1.0, 0.0, ALU.add, ALU.max))
                e.tensor_copy(ends_i[:, :], cum[:, :]).then_inc(s_v.sem, 1)
            on("vector")(vec1)

            def pe(e):
                e.wait_ge(s_v.sem, v0 + 1)
                e.matmul(pC[:, NB:2 * NB], ones[:, :], cnt[:, :], start=True, stop=True)
                e.matmul(pC[:, 2 * NB:3 * NB], upper[:, :], cnt[:, :], start=True, stop=True
                         ).then_inc(s_p.sem, 1)
            on("tensor")(pe)
            return v0 + 2

        def nodes(name, is_max, ends_ready):
            run_last = run[(CHUNKS - 1) % SLOTS]
            run_v = s_run[(CHUNKS - 1) % SLOTS].n
            tab = s_tab.n
            p0, v0 = s_p.n, s_v.n
            bump(s_p, 3)
            bump(s_v, 3)

            def vec_carry(e):
                e.wait_ge(s_run[(CHUNKS - 1) % SLOTS].sem, run_v)
                e.tensor_copy(state[:, :], run_last[:, T - 1, :]).then_inc(s_v.sem, 1)
                e.wait_ge(s_p.sem, p0 + 1)
                step(e, e.memset(state_row[:, 0:1], -BIG if is_max else 0.0))
                if is_max:
                    step(e, tt(e, state_row[:, 1:P], pT[0][0:D, 0:P - 1], row_m[:, 0, 1:P], ALU.mult))
                    step(e, tt(e, state_row[:, 1:P], state_row[:, 1:P], row_m[:, 3, 1:P], ALU.add))
                    step(e, e.tensor_tensor_scan(carry_row[:, :], row_m[:, 4, :], state_row[:, :], -BIG,
                                                 ALU.add, ALU.max))
                else:
                    step(e, tt(e, state_row[:, 1:P], pT[0][0:D, 0:P - 1], row_m[:, 0, 1:P], ALU.mult))
                    step(e, e.tensor_tensor_scan(carry_row[:, :], row_m[:, 2, :], state_row[:, :], 0.0,
                                                 ALU.mult, ALU.add))
                e.memset(sink[:, :], 0.0).then_inc(s_v.sem, 1)
                e.wait_ge(s_p.sem, p0 + 2)
                step(e, e.tensor_copy(carry[:, 0:D], pT[1][:, 0:D]))
                e.tensor_tensor(carry_hi[:, :, :], head_hi[:, :].unsqueeze(2).to_broadcast([P, NB, D]),
                                carry[:, 0:D].unsqueeze(1).to_broadcast([P, NB, D]),
                                ALU.mult).then_inc(s_v.sem, 1)
            on("vector")(vec_carry)

            rows_b = [c.n for c in s_rows]

            def pe(e):
                e.wait_ge(s_v.sem, v0 + 1)
                e.transpose(pT[0][0:D, 0:P], state[:, :], ident[:, :]).then_inc(s_p.sem, 1)
                e.wait_ge(s_v.sem, v0 + 2)
                e.transpose(pT[1][:, 0:D], carry_row[:, :], ident[0:D, 0:D]).then_inc(s_p.sem, 1)
                e.wait_ge(s_v.sem, v0 + 3)
                for s in range(SLOTS):
                    e.wait_ge(s_rows[s].sem, rows_b[s])
                flat = carry_hi[:, :, :].rearrange("p b d -> p (b d)")
                w = NB * D // 4
                for k in range(4):
                    e.matmul(pY[k // 2][:, k % 2, 0:w], head_lo[:, :], flat[:, k * w:(k + 1) * w],
                             start=True, stop=True)
                e.matmul(pY[0][:, 2, 0:NB], head_lo[:, :], head_hi[:, :], start=True, stop=True
                         ).then_inc(s_p.sem, 1)
            on("tensor")(pe)

            def chunk(e, i, s):
                flat = agg[:, :, :].rearrange("p b d -> p (b d)")
                e.tensor_copy(flat[:, bass.ds((i * SLOTS + s) * GB * D, GB * D)].rearrange("p (b d) -> p b d", d=D),
                              G[s][:, 0:GB, 0:D]).then_inc(s_free[s].sem, 1)
            gather(name, ends_i, {"act": [(s_v, ends_ready)], "pool": [(s_tab, tab)]},
                   scanned, D, GB, GB, GROUPS // SLOTS, chunk)

            taken = [c.n for c in s_free]

            def vec_fix(e):
                for s in range(SLOTS):
                    e.wait_ge(s_free[s].sem, taken[s])
                e.wait_ge(s_p.sem, p0 + 3)
                flat = agg[:, :, :].rearrange("p b d -> p (b d)")
                tflat = tmp[:, :, :].rearrange("p b d -> p (b d)")
                w = NB * D // 4
                if is_max:
                    step(e, e.tensor_scalar(stat[:, :], pY[0][:, 2, 0:NB], BIG, -BIG, ALU.mult, ALU.add))
                    for k in range(4):
                        ins = e.tensor_copy(tflat[:, k * w:(k + 1) * w], pY[k // 2][:, k % 2, 0:w])
                    step(e, ins)
                    step(e, tt(e, tmp[:, :, :], tmp[:, :, :], spread(stat[:, :]), ALU.add))
                    step(e, tt(e, agg[:, :, :], agg[:, :, :], tmp[:, :, :], ALU.max))
                else:
                    for k in range(4):
                        ins = tt(e, tflat[:, k * w:(k + 1) * w], flat[:, k * w:(k + 1) * w],
                                 pY[k // 2][:, k % 2, 0:w], ALU.add)
                    step(e, ins)
                    step(e, tt(e, agg[:, :, :], tmp[:, :, :], spread(has[:, :]), ALU.mult))
            on("vector")(vec_fix)

        def batch_norm(layer):
            p0, v0, a0 = s_p.n, s_v.n, s_a.n
            bump(s_p, 2)
            bump(s_v, 3)
            bump(s_a)
            per_feature = "p b d -> p d b"

            def pads_to_zero(e, t):
                step(e, e.tensor_scalar(t[:, NB - 1, :], t[:, NB - 1, :], real[:, 0:1], None, ALU.mult))

            def over_blocks(t):
                return t.unsqueeze(1).to_broadcast([P, NB, D])

            def vec(e):
                step(e, tt(e, agg[:, :, :], agg[:, :, :], root[:, :, :], ALU.add))
                pads_to_zero(e, agg)
                e.tensor_reduce(bn[:, 0, :], agg[:, :, :].rearrange(per_feature), AX.X, ALU.add
                                ).then_inc(s_v.sem, 1)
                e.wait_ge(s_p.sem, p0 + 1)
                step(e, e.tensor_scalar(bn[:, 1, :], pT[0][:, 0:D], 1.0 / N, None, ALU.mult))
                step(e, tt(e, agg[:, :, :], agg[:, :, :], over_blocks(bn[:, 1, :]), ALU.subtract))
                pads_to_zero(e, agg)
                step(e, tt(e, tmp[:, :, :], agg[:, :, :], agg[:, :, :], ALU.mult))
                e.tensor_reduce(bn[:, 0, :], tmp[:, :, :].rearrange(per_feature), AX.X, ALU.add
                                ).then_inc(s_v.sem, 1)
                e.wait_ge(s_p.sem, p0 + 2)
                e.tensor_scalar(bn[:, 1, :], pT[0][:, 0:D], 1.0 / N, BN_EPS, ALU.mult, ALU.add
                                ).then_inc(s_v.sem, 1)
                e.wait_ge(s_a.sem, a0 + 1)
                step(e, e.reciprocal(bn[:, 3, :], bn[:, 2, :]))
                step(e, tt(e, bn[:, 3, :], bn[:, 3, :], gamma[:, layer, :], ALU.mult))
                step(e, tt(e, tmp[:, :, :], agg[:, :, :], over_blocks(bn[:, 3, :]), ALU.mult))
                step(e, tt(e, tmp[:, :, :], tmp[:, :, :], over_blocks(beta[:, layer, :]), ALU.add))
                step(e, e.tensor_scalar(h[:, :, :], tmp[:, :, :], 0.0, None, ALU.max))
            on("vector")(vec)

            def pe(e):
                for k in range(2):
                    e.wait_ge(s_v.sem, v0 + 1 + k)
                    e.matmul(pT[0][:, 0:D], ones[:, :], bn[:, 0, :], start=True, stop=True
                             ).then_inc(s_p.sem, 1)
            on("tensor")(pe)

            def act(e):
                e.wait_ge(s_v.sem, v0 + 3)
                e.activation(bn[:, 2, :], bn[:, 1, :], ACT.Sqrt).then_inc(s_a.sem, 1)
            on("scalar")(act)
            publish_h()

        norm_relu()
        ends_ready = None
        for layer in range(LAYERS):
            if layer:
                prod = s_prod.n
                nxt = layer

                def load_w(e, prod=prod, nxt=nxt):
                    e.wait_ge(s_prod.sem, prod)
                    e.dma_start(conv_w[:, :], io["conv_w"][nxt]).then_inc(s_w.sem, 16)
                on("sync")(load_w)
                bump(s_w, 16)

            def conv_out(e, s, ps, g, k, m):
                e.tensor_copy(rows[s][:, k:k + m, :], ps[:, :, 0:ROW])
                flat = root[:, :, :].rearrange("p b d -> p (b d)")
                return e.tensor_copy(flat[:, bass.ds(g * (GB * D) + k * D, m * D)].rearrange(
                    "p (b d) -> p b d", d=D), ps[:, :, ROW:CW])
            v_parts = parts_of_h()
            node_product(conv_w, CW, conv_out, True,
                         (s_w, s_w.n) if layer else (s_in, IN_ALL))
            edges(f"conv{layer}", conv_table, ROW, io["attr"], EF, {"pool": [(s_tab, s_tab.n)],
                  "act": [(s_in, IN_ALL)]}, False, layer == 0, v_parts)
            if layer == 0:
                ends_ready = node_ends()
            nodes(f"end{layer}", False, ends_ready)
            if layer < LAYERS - 1:
                batch_norm(layer)
            else:
                def last_relu(e):
                    step(e, tt(e, agg[:, :, :], agg[:, :, :], root[:, :, :], ALU.add))
                    step(e, e.tensor_scalar(h[:, :, :], agg[:, :, :], 0.0, None, ALU.max))
                on("vector")(last_relu)
                publish_h()

        def residual_out(e, s, ps, g, k, m):
            flat = x[:, :, :].rearrange("p b d -> p (b d)")
            there = flat[:, bass.ds(g * (GB * D), GB * D)]
            return e.tensor_tensor(there, there, ps.rearrange("p b c -> p (b c)"), ALU.add)

        node_product(lin_w[:, 0, :], D, residual_out, False)
        all_rows = [c.n for c in s_rows]

        def order_x(e):
            for s in range(SLOTS):
                e.wait_ge(s_rows[s].sem, all_rows[s])
        on("vector")(order_x)

        norm_relu()
        h_ready = s_v.n
        v_parts = parts_of_h()
        max_stored = sem("s_max_table")

        def store_h(e):
            e.wait_ge(s_v.sem, h_ready)
            e.dma_start(max_table.rearrange("(b p) c -> p b c", p=P), h[:, :, :]).then_inc(max_stored.sem, 16)
        on("sync")(store_h)

        def to_max(e):
            step(e, e.tensor_scalar(same[:, :], same[:, :], BIG, -BIG, ALU.mult, ALU.add))
        on("vector")(to_max)
        edges("max", max_table, D, io["weight"], 1, {"pool": [(max_stored, 16)]}, True, False, v_parts)
        nodes("end_max", True, ends_ready)

        def take_agg(e):
            step(e, e.tensor_copy(h[:, :, :], agg[:, :, :]))
        on("vector")(take_agg)
        publish_h()
        node_product(lin_w[:, 1, :], D, residual_out, False)
        done = [c.n for c in s_rows]

        def write_out(e):
            for s in range(SLOTS):
                e.wait_ge(s_rows[s].sem, done[s])
            e.dma_start(io["out"], x[:, :, :]).then_inc(s_out.sem, 16)
            e.wait_ge(s_out.sem, 16)
        on("sync")(write_out)

        block = ctx.enter_context(nc.Block())

        def attach(decorate, name):
            @decorate
            def _(e):
                for f in programs[name]:
                    f(e)
        attach(block.sync, "sync")
        attach(block.gpsimd, "gpsimd")
        attach(block.scalar, "scalar")
        attach(block.vector, "vector")
        attach(block.tensor, "tensor")


def kernel(**inputs):
    import concourse.bacc as _bacc
    from concourse.bass_utils import run_bass_kernel_spmd as _run

    def streams(a, fill):
        a = np.asarray(a).reshape(E, -1)
        out = np.full((EPAD, a.shape[1]), fill, a.dtype)
        out[:E] = a
        return out.reshape(P, -1)

    def diagonal(blocks, width, bias):
        out = np.zeros((GB * D + 1, GB * width), np.float32)
        for b in range(GB):
            out[b * D:(b + 1) * D, b * width:(b + 1) * width] = blocks
            out[GB * D, b * width:(b + 1) * width] = bias
        return out

    f = {k: np.asarray(v) for k, v in inputs.items()}
    dst = streams(f["dst"], NPAD - 1)
    first, last = dst[:, 0], dst[:, -1]
    none = np.full(1, -1, dst.dtype)
    prev_last, prev_first = np.concatenate([none, last[:-1]]), np.concatenate([none, first[:-1]])
    next_first = np.concatenate([first[1:], none])

    x = np.zeros((NPAD, D), np.float32)
    x[:N] = f["x"]
    conv_w = []
    for layer in range(LAYERS):
        ew = f["L0_gnn_edge_w"][layer].reshape(EF, D, D).transpose(1, 0, 2).reshape(D, EF * D)
        eb = f["L0_gnn_edge_b"][layer].reshape(D, D)
        block = np.concatenate([ew, eb, f["L0_gnn_root_w"][layer]], axis=1)
        bias = np.concatenate([np.zeros(ROW, np.float32), f["L0_gnn_root_b"][layer]])
        conv_w.append(diagonal(block, CW, bias))
    lin_w = np.stack([diagonal(f["L0_gnn_pred_w"], D, f["L0_gnn_pred_b"]),
                      diagonal(f["L1_gnn_W"].T, D, f["L1_gnn_b"])], axis=1)
    order = np.arange(P)
    arrays = {
        "src": streams(f["src"], 0), "dst": dst, "attr": streams(f["edge_attr_8"], 0),
        "weight": streams(f["edge_weight1"], 0),
        "x": x.reshape(NB, P, D).transpose(1, 0, 2),
        "ident": np.eye(P, dtype=np.float32),
        "upper": (order[:, None] <= order[None, :]).astype(np.float32),
        "quarter_lane": (order[:, None] + P * np.arange(QUARTERS)).astype(np.float32),
        "far_mask": np.eye(FARS, dtype=np.float32).astype(mybir.dt.np(BF16))[:, :, None].repeat(D, 2),
        "pe_src": streams(f["src"], 0).reshape(P, CHUNKS, T)[:, :, TG:].transpose(1, 2, 0).reshape(
            CHUNKS, PE_EDGES),
        "lanes": np.broadcast_to(order.astype(np.float32), (P, P)),
        "real": (order < LAST).astype(np.float32)[:, None],
        "lin_w": lin_w, "conv_w": np.stack(conv_w),
        "gamma": np.broadcast_to(f["L0_gnn_bn_gamma"], (P, LAYERS - 1, D)),
        "beta": np.broadcast_to(f["L0_gnn_bn_beta"], (P, LAYERS - 1, D)),
        "borders": np.stack([first, last, prev_last, next_first], axis=1),
        "borders_row": np.broadcast_to(np.stack([first, prev_last, prev_first]), (D, 3, P)),
    }
    nc = _bacc.Bacc("TRN2", target_bir_lowering=False, num_devices=1)
    arrays = {f"in_{k}": np.ascontiguousarray(v) for k, v in arrays.items()}
    io = {k[3:]: nc.dram_tensor(k, v.shape, mybir.dt.from_np(v.dtype), kind="ExternalInput").ap()
          for k, v in arrays.items()}
    io["out"] = nc.dram_tensor("out", (P, NB, D), F32, kind="ExternalOutput").ap()
    build(nc, io)
    got = _run(nc, [arrays], core_ids=[0]).results[0]["out"]
    return np.asarray(got).transpose(1, 0, 2).reshape(NPAD, D)[:N]
```

```python
import numpy as np
import concourse.bass as bass
from concourse import mybir
from contextlib import ExitStack

F32, BF16, F16, I32 = mybir.dt.float32, mybir.dt.bfloat16, mybir.dt.float16, mybir.dt.int32
ALU = mybir.AluOpType
ACT = mybir.ActivationFunctionType
AX = mybir.AxisListType

P = 128
N, D, EF, E, LAYERS = 12500, 16, 8, 412500, 3
FB = EF + 1
ROW = FB * D
NB = -(-N // P)
NPAD = NB * P
LAST = N - (NB - 1) * P
T = 26
CHUNKS = 124
STREAM = T * CHUNKS
EPAD = P * STREAM
SLOTS = 2
GB = 7
GROUPS = NB // GB
CW = ROW + D
PER_BANK = 512 // CW
TP = 8
TG = T - TP
ZONES = 7
NEAR = NB // ZONES
BANKS = 4
HEAD = 3
W0, W1, W2 = 104, 64, 62
PE_EDGES = TP * P
FAR = 2.0 ** 126
BIG = 1.5e38
LN_EPS = BN_EPS = 1e-5
assert EPAD >= E and E > (P - 1) * STREAM and GROUPS * GB == NB and GROUPS % SLOTS == 0
assert CHUNKS % SLOTS == 0 and CHUNKS <= P and ZONES * NEAR == NB
assert SLOTS * TP % BANKS == 0 and W0 * W1 * W2 == EPAD and STREAM % W2 == 0


class Count:
    def __init__(self, sem):
        self.sem, self.n = sem, 0


def build(nc, io):
    ctx = ExitStack()

    def sb(name, shape, dt=F32):
        return ctx.enter_context(nc.sbuf_tensor(name, shape, dt))

    def sem(name):
        return Count(ctx.enter_context(nc.semaphore(name)))

    def slots(make, name, *a):
        return [make(f"{name}{s}", *a) for s in range(SLOTS)]

    with ctx:
        conv_table = nc.dram_tensor("conv_table", (NPAD, ROW), F32, kind="Internal").ap()
        max_table = nc.dram_tensor("max_table", (NPAD, D), F32, kind="Internal").ap()
        scanned = nc.dram_tensor("scanned", (EPAD, D), F32, kind="Internal").ap()
        key_rows = nc.dram_tensor("key_rows", (CHUNKS, PE_EDGES), F16, kind="Internal").ap()
        near_rows = nc.dram_tensor("near_rows", (CHUNKS, PE_EDGES), F16, kind="Internal").ap()
        conv_rows = conv_table.rearrange("(b p) c -> p b c", p=P)
        scanned_rows = scanned.rearrange("(p t) c -> p (t c)", p=P)

        src = sb("src", [P, STREAM], I32)
        dst = sb("dst", [P, STREAM], I32)
        same = sb("same", [P, STREAM])
        x = sb("x_res", [P, NB, D])
        h = sb("h", [P, NB, D])
        agg = sb("agg", [P, NB, D])
        root = sb("root", [P, NB, D])
        tmp = sb("tmp", [P, NB, D])
        ident = sb("ident", [P, P])
        ones = sb("ones", [P, P])
        lanes = sb("lanes", [P, P])
        real = sb("real", [P, 1])
        conv_w = sb("conv_w", [GB * D + 1, GB * CW])
        lin_w = sb("lin_w", [GB * D + 1, 2, GB * D])
        gamma = sb("gamma", [P, LAYERS - 1, D])
        beta = sb("beta", [P, LAYERS - 1, D])
        ends_i = sb("ends_i", [P, NB], I32)
        rank = sb("rank", [P, 3, NB])
        rank_i = sb("rank_i", [P, NB], I32)
        node_id = sb("node_id", [P, NB])
        row_first = sb("row_first", [P, W0], I32)
        edge_w = sb("edge_w", [TP * D, TP * ROW])
        stat = sb("stat", [P, NB])
        stat2 = sb("stat2", [P, NB])
        bn = sb("bn", [P, 4, D])
        sink = sb("sink", [P, 1])
        edge_i = sb("edge_i", [P, 4], I32)
        edge_m = sb("edge_m", [P, 6])
        head_lo = sb("head_lo", [P, P])
        head_hi = sb("head_hi", [P, NB])
        head_lo_i = sb("head_lo_i", [P, 2], I32)
        row_i = sb("row_i", [D, 3, P], I32)
        row_m = sb("row_m", [D, 6, P])
        state = sb("state", [P, D])
        state_row = sb("state_row", [D, P])
        carry_row = sb("carry_row", [D, P])
        carry = sb("carry", [P, D + 1])
        carry_hi = sb("carry_hi", [P, NB, D])

        idx = slots(sb, "idx", [P, T], I32)
        G = slots(sb, "gathered", [P, T, ROW])
        attr = slots(sb, "attr", [P, T, EF])
        msg = sb("msg", [P, T, D])
        run = slots(sb, "run", [P, T, D])
        parts = [sb(f"part{k}", [P, NB, D], BF16) for k in range(3)]
        zone_lane = sb("zone_lane", [P, ZONES])
        near_mask = sb("near_mask", [NEAR, NEAR, D], BF16)
        keys = slots(sb, "keys", [P, PE_EDGES], F16)
        nears = slots(sb, "nears", [NEAR, PE_EDGES], F16)
        hot_key = slots(sb, "hot_key", [P, ZONES, PE_EDGES], BF16)
        not_near = slots(sb, "not_near", [NEAR, PE_EDGES], BF16)
        xe = slots(sb, "xe", [P, TP * D])
        xeT = sb("xeT", [TP * D, P])
        pe_src = sb("pe_src", [CHUNKS, PE_EDGES], I32)
        pe_tmp = sb("pe_tmp", [CHUNKS, PE_EDGES], I32)
        hs = slots(sb, "hs", [P, GB * D + 1])
        hT = slots(sb, "hT", [GB * D + 1, P])
        rows = slots(sb, "rows", [P, GB, ROW])

        pT = [ctx.enter_context(nc.psum_tensor(f"pT{s}", [P, 512], F32)) for s in range(SLOTS)]
        pY = [ctx.enter_context(nc.psum_tensor(f"pY{s}", [P, 3, 512], F32)) for s in range(SLOTS)]
        pE = pY[0]
        pG = [b[:, 0:NEAR * D] for b in (pY[1][:, 0, :], pY[1][:, 1, :], pY[1][:, 2, :], pT[1])]

        s_first = sem("s_first")
        s_in = sem("s_in")
        s_w = sem("s_w")
        s_init = sem("s_init")
        s_free = slots(sem, "s_free")
        s_idx = slots(sem, "s_idx")
        s_run = slots(sem, "s_run")
        s_runfree = slots(sem, "s_runfree")
        s_step = sem("s_step")
        s_found = sem("s_found")
        s_hs = slots(sem, "s_hs")
        s_tr = slots(sem, "s_tr")
        s_hT = slots(sem, "s_hT")
        s_mm = slots(sem, "s_mm")
        s_rows = slots(sem, "s_rows")
        s_rowsfree = slots(sem, "s_rowsfree")
        s_keys = sem("s_keys")
        s_hotk = slots(sem, "s_hotk")
        s_gath = sem("s_gath")
        s_pick = sem("s_pick")
        s_xt = sem("s_xt")
        s_xeT = sem("s_xeT")
        s_prod = sem("s_prod")
        s_rowsG = slots(sem, "s_rowsG")
        s_v = sem("s_v")
        s_p = sem("s_p")
        s_a = sem("s_a")
        s_tab = sem("s_tab")
        s_out = sem("s_out")
        tick = {e: sem(f"s_tick_{e}") for e in ("pool", "act", "sp")}

        programs = {e: [] for e in ("sync", "gpsimd", "scalar", "vector", "tensor")}

        def on(engine):
            return programs[engine].append

        def gate(eng, who, s, value):
            eng.wait_ge(s.sem, value)
            if who in ("pool", "act", "sp"):
                eng.sem_inc(tick[who].sem, 1)

        def bump(s, n=1):
            s.n += n
            return s.n

        first_loads = [(node_id, io["node_id"]), (row_first, io["row_first"]), (x, io["x"]),
                       (ident, io["ident"]), (conv_w, io["conv_w"][0])]
        loads = [(pe_src, io["pe_src"]), (dst, io["dst"]), (src, io["src"]), (lanes, io["lanes"]),
                 (real, io["real"]), (lin_w, io["lin_w"]), (gamma, io["gamma"]), (beta, io["beta"]),
                 (edge_i, io["borders"]), (zone_lane, io["zone_lane"]), (near_mask, io["near_mask"]),
                 (row_i, io["borders_row"]), (edge_w, io["edge_w"][0])]

        def sync_start(e):
            for lot, s in ((first_loads, s_first), (loads, s_in)):
                for tile, ap in lot:
                    e.dma_start(tile[tuple(slice(None) for _ in tile.shape)], ap).then_inc(s.sem, 16)
        on("sync")(sync_start)
        bump(s_in, 16 * len(loads))
        IN_ALL = s_in.n
        FIRST_ALL = bump(s_first, 16 * len(first_loads))

        def step(e, ins):
            ins.then_inc(s_step.sem, 1)
            s_step.n += 1
            e.wait_ge(s_step.sem, s_step.n)

        def tt(e, out, a, b, op):
            return e.tensor_tensor(out, a, b, op)

        INIT_ALL = 2 + 2 * SLOTS

        src_f, zone_f = (g[0:CHUNKS, :, :].rearrange("p t c -> p (t c)")[:, 0:PE_EDGES] for g in G)

        def vector_start(e):
            e.memset(ones[:, :], 1.0).then_inc(s_init.sem, 1)
            for s in range(SLOTS):
                e.memset(hs[s][:, :], 1.0).then_inc(s_init.sem, 1)
                e.memset(run[s][:, :, :], 0.0).then_inc(s_init.sem, 1)
                e.memset(G[s][:, 0, 0:1], 0.0).then_inc(s_free[s].sem, 1)
            e.memset(carry[:, D:D + 1], 1.0).then_inc(s_init.sem, 1)
            e.wait_ge(s_first.sem, FIRST_ALL)
            e.wait_ge(s_init.sem, INIT_ALL)

        def vector_masks(e):
            e.wait_ge(s_in.sem, IN_ALL)
            step(e, e.memset(same[:, 0:1], 0.0))
            e.tensor_tensor(same[:, 1:STREAM], dst[:, 1:STREAM], dst[:, 0:STREAM - 1], ALU.is_equal)
            first, last, prev_last, next_first = (edge_i[:, k:k + 1] for k in range(4))
            tt(e, edge_m[:, 0:1], first, prev_last, ALU.is_equal)
            tt(e, edge_m[:, 1:2], first, last, ALU.is_equal)
            step(e, tt(e, edge_m[:, 2:3], next_first, last, ALU.is_equal))
            step(e, tt(e, edge_m[:, 3:4], edge_m[:, 1:2], edge_m[:, 2:3], ALU.mult))
            step(e, e.tensor_scalar(edge_m[:, 4:5], edge_m[:, 3:4], -1.0, 1.0, ALU.mult, ALU.add))
            e.tensor_scalar(head_lo_i[:, 0:1], first, P - 1, None, ALU.bitwise_and)
            step(e, e.tensor_scalar(head_lo_i[:, 1:2], first, 7, None, ALU.logical_shift_right))
            step(e, e.tensor_copy(edge_m[:, 0:2], head_lo_i[:, 0:2]))
            step(e, e.tensor_scalar(head_lo[:, :], lanes[:, :], edge_m[:, 0:1], edge_m[:, 4:5],
                                    ALU.is_equal, ALU.mult))
            step(e, e.tensor_scalar(head_hi[:, :], lanes[:, 0:NB], edge_m[:, 1:2], None, ALU.is_equal))
            rf, rpl, rpf = (row_i[:, k, :] for k in range(3))
            tt(e, row_m[:, 0, :], rf, rpl, ALU.is_equal)
            step(e, tt(e, row_m[:, 1, :], rpf, rpl, ALU.is_equal))
            step(e, tt(e, row_m[:, 2, :], row_m[:, 0, :], row_m[:, 1, :], ALU.mult))
            e.tensor_scalar(row_m[:, 3, :], row_m[:, 0, :], BIG, -BIG, ALU.mult, ALU.add)
            step(e, e.tensor_scalar(row_m[:, 4, :], row_m[:, 2, :], BIG, -BIG, ALU.mult, ALU.add))
            step(e, e.tensor_copy(src_f, pe_src[:, :]))
            step(e, e.tensor_scalar(zone_f, src_f, float(NEAR * P), None, ALU.is_ge))
            for z in range(2, ZONES):
                step(e, e.scalar_tensor_tensor(zone_f, src_f, float(z * NEAR * P), zone_f, ALU.is_ge, ALU.add))
            step(e, e.scalar_tensor_tensor(pe_tmp[:, :], zone_f, -float(NEAR * P), src_f, ALU.mult, ALU.add))
            step(e, e.tensor_scalar(pe_tmp[:, :], pe_tmp[:, :], 7, None, ALU.logical_shift_right))
            step(e, e.tensor_copy(keys[1][0:CHUNKS, :], pe_tmp[:, :]))
            step(e, e.tensor_scalar(pe_src[:, :], pe_src[:, :], P - 1, None, ALU.bitwise_and))
            e.scalar_tensor_tensor(keys[0][0:CHUNKS, :], zone_f, float(P), pe_src[:, :], ALU.mult,
                                   ALU.add).then_inc(s_v.sem, 1)
        on("vector")(vector_start)

        def masks_and_keys():
            on("vector")(vector_masks)
            v = bump(s_v)

            def sync_keys(e):
                e.wait_ge(s_v.sem, v)
                for ap, half in ((key_rows, keys[0]), (near_rows, keys[1])):
                    e.dma_start(ap, half[0:CHUNKS, :]).then_inc(s_keys.sem, 16)
                e.wait_ge(s_keys.sem, 32)
            on("sync")(sync_keys)

        def credits(name, engine, counts):
            def f(e):
                for c in counts:
                    e.sem_inc(c.sem, 1)
            on(engine)(f)
            for c in counts:
                c.n = 1
        for c in s_free:
            c.n = 1
        credits("sp", "sync", s_runfree + s_rowsfree)
        credits("pe", "tensor", s_tr + s_mm + [s_prod])
        credits("act", "scalar", s_rowsG)
        credits("dve", "vector", [s_pick] * BANKS)
        s_pick.n = BANKS
        credits("dve", "vector", s_rows)
        for c in s_rows:
            c.n = 1

        def spread(t):
            return t.unsqueeze(2).to_broadcast([P, NB, D])

        def norm_relu():
            a0 = s_a.n
            bump(s_a)
            bump(s_v)
            v0 = s_v.n

            def vec(e):
                step(e, e.tensor_reduce(stat[:, :], x[:, :, :], AX.X, ALU.add))
                step(e, e.tensor_scalar(stat[:, :], stat[:, :], 1.0 / D, None, ALU.mult))
                step(e, tt(e, h[:, :, :], x[:, :, :], spread(stat[:, :]), ALU.subtract))
                step(e, tt(e, tmp[:, :, :], h[:, :, :], h[:, :, :], ALU.mult))
                step(e, e.tensor_reduce(stat2[:, :], tmp[:, :, :], AX.X, ALU.add))
                e.tensor_scalar(stat2[:, :], stat2[:, :], 1.0 / D, LN_EPS, ALU.mult,
                                ALU.add).then_inc(s_v.sem, 1)
                e.wait_ge(s_a.sem, a0 + 1)
                step(e, e.reciprocal(stat2[:, :], stat[:, :]))
                step(e, tt(e, tmp[:, :, :], h[:, :, :], spread(stat2[:, :]), ALU.mult))
                step(e, e.tensor_scalar(h[:, :, :], tmp[:, :, :], 0.0, None, ALU.max))
            on("vector")(vec)

            def act(e):
                e.wait_ge(s_v.sem, v0)
                e.activation(stat[:, :], stat2[:, :], ACT.Sqrt).then_inc(s_a.sem, 1)
            on("scalar")(act)
            publish_h()

        def publish_h():
            bump(s_v)
            on("vector")(lambda e: e.memset(sink[:, :], 0.0).then_inc(s_v.sem, 1))

        def node_product(weights, width, out_fn, store, wait_weights=None):
            v_ready = s_v.n
            b = {k: [c.n for c in cs] for k, cs in
                 dict(hs=s_hs, tr=s_tr, hT=s_hT, mm=s_mm, rows=s_rows, rf=s_rowsfree).items()}
            per_bank = 512 // width if width * GB > 512 else GB
            pieces = [(k, min(per_bank, GB - k)) for k in range(0, GB, per_bank)]
            store_sems = slots(sem, f"s_store{len(programs['sync'])}_") if store else None

            it = GROUPS // SLOTS

            def act_stage(e, i, s):
                hf = h[:, :, :].rearrange("p b d -> p (b d)")
                e.copy(hs[s][:, 0:GB * D], hf[:, bass.ds((i * SLOTS + s) * GB * D, GB * D)]
                       ).then_inc(s_hs[s].sem, 1)

            def act_pair(e, i, more):
                for s in range(SLOTS):
                    gate(e, "act", s_tr[s], i + (b["tr"][s] + 1))
                    if more:
                        act_stage(e, i + 1, s)
                    gate(e, "act", s_mm[s], i + b["mm"][s])
                    e.copy(hT[s][:, :], pT[s][0:GB * D + 1, 0:P]).then_inc(s_hT[s].sem, 1)

            def act(e):
                e.wait_ge(s_v.sem, v_ready)
                for s in range(SLOTS):
                    e.wait_ge(s_tr[s].sem, b["tr"][s])
                    act_stage(e, 0, s)
                with e.Fori(0, it - 1) as i:
                    act_pair(e, i, True)
                act_pair(e, it - 1, False)
            on("scalar")(act)

            def pe_turn(e, i, s):
                gate(e, "pe", s_hs[s], i + (b["hs"][s] + 1))
                e.transpose(pT[s][0:GB * D + 1, 0:P], hs[s][:, :], ident[:, :]).then_inc(s_tr[s].sem, 1)

            def pe_pair(e, i, more):
                for s in range(SLOTS):
                    gate(e, "pe", s_hT[s], i + (b["hT"][s] + 1))
                    if more:
                        pe_turn(e, i + 1, s)
                    gate(e, "pe", s_rows[s], i + b["rows"][s])
                    for n, (k, m) in enumerate(pieces):
                        ins = e.matmul(pY[s][:, n, 0:m * width], hT[s][:, :],
                                       weights[:, k * width:(k + m) * width], start=True, stop=True)
                    ins.then_inc(s_mm[s].sem, 1)

            def pe(e):
                if wait_weights is not None:
                    e.wait_ge(wait_weights[0].sem, wait_weights[1])
                for s in range(SLOTS):
                    pe_turn(e, 0, s)
                with e.Fori(0, it - 1) as i:
                    pe_pair(e, i, True)
                pe_pair(e, it - 1, False)
            on("tensor")(pe)

            def vec(e):
                with e.Fori(0, it) as i:
                    for s in range(SLOTS):
                        gate(e, "dve", s_mm[s], i + b["mm"][s] + 1)
                        if store:
                            gate(e, "dve", s_rowsfree[s], i + b["rf"][s])
                        for n, (k, m) in enumerate(pieces):
                            ps = pY[s][:, n, 0:m * width].rearrange("p (b c) -> p b c", c=width)
                            ins = out_fn(e, s, ps, i * SLOTS + s, k, m)
                        ins.then_inc(s_rows[s].sem, 1)
            on("vector")(vec)

            if store:
                def sp(e):
                    with e.Fori(0, it) as i:
                        for s in range(SLOTS):
                            gate(e, "sp", s_rows[s], i + b["rows"][s] + 1)
                            e.dma_start(conv_rows[:, bass.ds((i * SLOTS + s) * GB, GB), :],
                                        rows[s][:, :, :]).then_inc(store_sems[s].sem, 16)
                        for s in range(SLOTS):
                            gate(e, "sp", store_sems[s], i * 16 + 16)
                            e.sem_inc(s_rowsfree[s].sem, 1)
                    e.sem_inc(s_tab.sem, 1)
                on("sync")(sp)
                bump(s_tab)
            for cs in (s_hs, s_tr, s_hT, s_mm, s_rows) + ((s_rowsfree,) if store else ()):
                for c in cs:
                    bump(c, it)

        def pool_gather(name, table, width, steps, iters, ready):
            got = slots(sem, f"s_got_{name}")
            b_idx = [c.n for c in s_idx]

            def pool(e):
                for c, v in ready:
                    e.wait_ge(c.sem, v)
                with e.Fori(0, iters) as i:
                    for s in range(SLOTS):
                        gate(e, "pool", s_idx[s], i + (b_idx[s] + 1))
                        for t in range(steps):
                            e.indirect_dma_start(
                                out=G[s][:, t, 0:width], out_offset=None, in_=table[:, :],
                                in_offset=bass.IndirectOffsetOnAxis(ap=idx[s][:, t:t + 1], axis=0)
                            ).then_inc(got[s].sem, 16)
            on("gpsimd")(pool)
            for c in s_free + s_idx:
                bump(c, iters)
            return got

        def node_gather(name, indices, indices_ready, table, width, ready, vec_group):
            b_free = [c.n for c in s_free]
            iters = GROUPS // SLOTS

            def act(e):
                e.wait_ge(s_v.sem, indices_ready)
                with e.Fori(0, iters) as i:
                    for s in range(SLOTS):
                        gate(e, "act", s_free[s], i + b_free[s])
                        e.copy(idx[s][:, 0:GB], indices[:, bass.ds((i * SLOTS + s) * GB, GB)]
                               ).then_inc(s_idx[s].sem, 1)
            on("scalar")(act)
            got = pool_gather(name, table, width, GB, iters, ready)

            def vec(e):
                with e.Fori(0, iters) as i:
                    for s in range(SLOTS):
                        gate(e, "dve", got[s], (i + 1) * (16 * GB))
                        vec_group(e, i, s)
            on("vector")(vec)

        def load_keys(e, keyed, n, s):
            for tile, ap, parts_n in ((keys[s], key_rows, P), (nears[s], near_rows, NEAR)):
                e.dma_start(tile[:, :], ap[bass.ds(n, 1), :].to_broadcast([parts_n, PE_EDGES])
                            ).then_inc(keyed[s].sem, 16)

        def hots(e, keyed, i, s, between=lambda: None):
            gate(e, "dve", keyed[s], i * 32 + 32)
            for z in range(ZONES):
                e.tensor_scalar(hot_key[s][:, z, :], keys[s][:, :], zone_lane[:, z:z + 1], None,
                                ALU.is_equal)
                if z == ZONES // 2:
                    between()
            e.tensor_scalar(not_near[s][:, :], nears[s][:, :], zone_lane[0:NEAR, 0:1], -FAR,
                            ALU.not_equal, ALU.mult).then_inc(s_hotk[s].sem, 1)

        def first_hots(name):
            keyed = slots(sem, f"s_keyed_{name}")
            b_hotk = [c.n for c in s_hotk]

            def sp(e):
                for s in range(SLOTS):
                    if b_hotk[s]:
                        e.wait_ge(s_hotk[s].sem, b_hotk[s])
                    load_keys(e, keyed, s, s)
                for s in range(SLOTS):
                    e.wait_ge(s_hotk[s].sem, b_hotk[s] + 1)
                    load_keys(e, keyed, SLOTS + s, s)
            on("sync")(sp)

            def vec(e):
                for s in range(SLOTS):
                    hots(e, keyed, 0, s)
            on("vector")(vec)
            return keyed

        def edges(name, table, width, attr_dram, attr_width, ready, is_max, v_parts, keyed):
            iters = CHUNKS // SLOTS
            b_free, b_run, b_rf, b_hotk, b_rg = (
                [c.n for c in cs] for cs in (s_free, s_run, s_runfree, s_hotk, s_rowsG))
            b_gath, b_pick, b_xt, b_xeT, b_prod = (c.n for c in (s_gath, s_pick, s_xt, s_xeT, s_prod))
            loaded = slots(sem, f"s_attr_{name}")
            stored = slots(sem, f"s_stored_{name}")

            def next_keys(e, i, s):
                gate(e, "sp", s_hotk[s], i + b_hotk[s])
                load_keys(e, keyed, i * SLOTS + s, s)

            def sp_pair(e, i, more_keys):
                for s in range(SLOTS):
                    gate(e, "sp", s_free[s], i + b_free[s])
                    e.dma_start(attr[s][:, :, 0:attr_width].rearrange("p t f -> p (t f)")
                                if attr_width == EF else attr1[s],
                                attr_dram[:, bass.ds((i * SLOTS + s) * T * attr_width, T * attr_width)]
                                ).then_inc(loaded[s].sem, 16)
                for s in range(SLOTS):
                    if more_keys:
                        next_keys(e, i + 2, s)
                    gate(e, "sp", s_run[s], i + b_run[s] + 1)
                    e.dma_start(scanned_rows[:, bass.ds((i * SLOTS + s) * T * D, T * D)],
                                run[s][:, :, :].rearrange("p t d -> p (t d)")).then_inc(stored[s].sem, 16)
                for s in range(SLOTS):
                    gate(e, "sp", stored[s], i * 16 + 16)
                    e.sem_inc(s_runfree[s].sem, 1)

            def sp(e):
                with e.Fori(0, iters - 2) as i:
                    sp_pair(e, i, True)
                for i in (iters - 2, iters - 1):
                    sp_pair(e, i, False)
                e.sem_inc(s_tab.sem, 1)
            on("sync")(sp)
            bump(s_tab)

            def after(i, s):
                return (i, 1) if s == 0 else (i + 1, 0)

            def pe_step(e, i, s, j):
                g = s * TP + j
                bank = g % BANKS
                gate(e, "pe", s_pick, i * (SLOTS * TP) + (b_pick + g - BANKS + 1))
                for z in range(ZONES):
                    for k, part in enumerate(parts):
                        e.matmul(pG[bank], hot_key[s][:, z, j * P:(j + 1) * P],
                                 part[:, z * NEAR:(z + 1) * NEAR, :], start=(z == 0 and k == 0), stop=False)
                e.matmul(pG[bank], not_near[s][:, j * P:(j + 1) * P], near_mask[:, :, :],
                         start=False, stop=True).then_inc(s_gath.sem, 1)

            def pe_body(e, i, s, more):
                o = 1 - s
                ni, ns = after(i, s)
                n = i * SLOTS + s
                for j in range(HEAD, TP):
                    pe_step(e, i, s, j)
                if more:
                    gate(e, "pe", s_hotk[ns], ni + (b_hotk[ns] + 1))
                    for j in range(HEAD - 1):
                        pe_step(e, ni, ns, j)
                if not is_max:
                    gate(e, "pe", s_pick, n * TP + (TP + b_pick))
                    e.transpose(pT[0][0:TP * D, 0:P], xe[s][:, :], ident[:, :]).then_inc(s_xt.sem, 1)
                if more:
                    pe_step(e, ni, ns, HEAD - 1)
                if not is_max:
                    gate(e, "pe", s_xeT, n + (1 + b_xeT))
                    gate(e, "pe", s_rowsG[o], i + (b_rg[o] + s))
                    for k, m in PE_PIECES:
                        ins = e.matmul(pE[:, k // 3, 0:m * ROW], xeT[:, :], edge_w[:, k * ROW:(k + m) * ROW],
                                       start=True, stop=True)
                    ins.then_inc(s_prod.sem, 1)

            rows_taken = [c.n for c in s_rows]

            def pe(e):
                e.wait_ge(s_v.sem, v_parts)
                for s in range(SLOTS):
                    e.wait_ge(s_rows[s].sem, rows_taken[s])
                e.wait_ge(s_hotk[0].sem, b_hotk[0] + 1)
                for j in range(HEAD):
                    pe_step(e, 0, 0, j)
                with e.Fori(0, iters - 1) as i:
                    for s in range(SLOTS):
                        pe_body(e, i, s, True)
                for s in range(SLOTS):
                    pe_body(e, iters - 1, s, s == 0)
            on("tensor")(pe)

            def act_rows(e, i, s):
                n = i * SLOTS + s
                gate(e, "act", s_free[s], i + b_free[s])
                if is_max:
                    gate(e, "act", s_pick, n * TP + (TP + b_pick))
                    e.copy(G[s][:, TG:T, 0:D], xe[s][:, :].rearrange("p (t d) -> p t d", d=D)
                           ).then_inc(s_rowsG[s].sem, 1)
                    return
                gate(e, "act", s_xt, n + (1 + b_xt))
                gate(e, "act", s_prod, n + b_prod)
                e.copy(xeT[:, :], pT[0][0:TP * D, 0:P]).then_inc(s_xeT.sem, 1)
                gate(e, "act", s_prod, n + (1 + b_prod))
                for k, m in PE_PIECES:
                    ins = e.copy(G[s][:, TG + k:TG + k + m, :],
                                 pE[:, k // 3, 0:m * ROW].rearrange("p (t c) -> p t c", c=ROW))
                ins.then_inc(s_rowsG[s].sem, 1)

            def pick(e, i, s, j):
                g = s * TP + j
                gate(e, "dve", s_gath, i * (SLOTS * TP) + (b_gath + g + 1))
                e.tensor_reduce(xe[s][:, j * D:(j + 1) * D], pG[g % BANKS].rearrange("p (r d) -> p d r", d=D),
                                AX.X, ALU.max).then_inc(s_pick.sem, 1)

            MARKS = 1 if is_max else 3
            base = [0]

            def body(e, i, s, hot, pick_next, pick_head, got):
                n = i * SLOTS + s
                ni, ns = after(i, s)
                marks = [0]

                def mark(ins):
                    ins.then_inc(s_step.sem, 1)
                    marks[0] += 1
                    return marks[0]

                def release(i, s):
                    if hot:
                        indices(e, i + 1, s)
                    e.sem_inc(s_free[s].sem, 1)

                def need(k):
                    gate(e, "dve", s_step, n * MARKS + (base[0] + k))

                def pick_rest(j):
                    if pick_next:
                        pick(e, ni, ns, j)

                def pick_rests(a, b):
                    for j in range(a, b):
                        pick_rest(j)

                def pick_first(j):
                    if pick_head:
                        pick(e, i + 1, s, j)

                if hot:
                    hots(e, keyed, i + 1, s, lambda: pick_rest(3))
                else:
                    pick_rest(3)
                pick_rest(4)
                gate(e, "dve", got[s], i * (16 * TG) + 16 * TG)
                gate(e, "dve", loaded[s], i * 16 + 16)
                g = G[s]
                if is_max:
                    gate(e, "dve", s_rowsG[s], i + (b_rg[s] + 1))
                    m_all = mark(tt(e, msg[:, :, :], g[:, :, 0:D],
                                    attr1[s].unsqueeze(2).to_broadcast([P, T, D]), ALU.mult))
                    pick_rest(5)
                    need(m_all)
                    release(i, s)
                    pick_rests(6, TP)
                    pick_first(0)
                else:
                    def product(a, b):
                        g4 = g[:, a:b, 0:EF * D].rearrange("p t (f d) -> p t f d", d=D)
                        return mark(tt(e, g4, g4, attr[s][:, a:b, :].unsqueeze(3).to_broadcast(
                            [P, b - a, EF, D]), ALU.mult))

                    def total(a, b):
                        return e.tensor_reduce(msg[:, a:b, :], g[:, a:b, :].rearrange(
                            "p t (f d) -> p t d f", d=D), AX.X, ALU.add)
                    half = T // 2
                    m_a = product(0, half)
                    pick_rest(5)
                    gate(e, "dve", s_rowsG[s], i + (b_rg[s] + 1))
                    m_b = product(half, T)
                    pick_rest(6)
                    need(m_a)
                    total(0, half)
                    pick_rest(7)
                    need(m_b)
                    m_all = mark(total(half, T))
                    need(m_all)
                    release(i, s)
                    pick_first(0)
                gate(e, "dve", s_runfree[s], i + b_rf[s])
                flags = same[:, bass.ds(n * T, T)]
                for d in range(D):
                    ins = e.tensor_tensor_scan(run[s][:, :, d], flags, msg[:, :, d],
                                               run[1 - s][:, T - 1, d:d + 1],
                                               ALU.add if is_max else ALU.mult,
                                               ALU.max if is_max else ALU.add)
                    if d == D - 1:
                        ins.then_inc(s_run[s].sem, 1)
                    if d % 8 == 7:
                        pick_first(1 + d // 8)
                gate(e, "dve", s_run[s], i + (b_run[s] + 1))
                assert marks[0] == MARKS

            def act(e):
                with e.Fori(0, iters) as i:
                    for s in range(SLOTS):
                        act_rows(e, i, s)
            on("scalar")(act)
            got = pool_gather(name, table, width, TG, iters, ready)

            def indices(e, i, s):
                return e.tensor_scalar(idx[s][:, 0:TG], src[:, bass.ds((i * SLOTS + s) * T, TG)],
                                       0.0, None, ALU.add).then_inc(s_idx[s].sem, 1)

            def vec(e):
                base[0] = s_step.n
                for s in range(SLOTS):
                    e.wait_ge(s_free[s].sem, b_free[s])
                    indices(e, 0, s)
                for j in range(TP):
                    pick(e, 0, 0, j)
                for j in range(HEAD):
                    pick(e, 0, 1, j)
                with e.Fori(0, iters - 1) as i:
                    for s in range(SLOTS):
                        body(e, i, s, True, True, True, got)
                body(e, iters - 1, 0, False, True, False, got)
                body(e, iters - 1, 1, False, False, False, got)
                s_step.n += MARKS * CHUNKS
            on("vector")(vec)
            for cc in s_run + s_runfree + s_hotk + s_rowsG:
                bump(cc, iters)
            for cc in (s_gath, s_pick):
                bump(cc, CHUNKS * TP)
            if not is_max:
                for cc in (s_xt, s_xeT, s_prod):
                    bump(cc, CHUNKS)

        PE_PIECES = [(k, min(3, TP - k)) for k in range(0, TP, 3)]

        def parts_of_h():
            v = bump(s_v)

            def vec(e):
                step(e, e.tensor_copy(parts[0][:, 0:NB, :], h[:, :, :]))
                step(e, tt(e, tmp[:, :, :], h[:, :, :], parts[0][:, 0:NB, :], ALU.subtract))
                step(e, e.tensor_copy(parts[1][:, 0:NB, :], tmp[:, :, :]))
                step(e, tt(e, tmp[:, :, :], tmp[:, :, :], parts[1][:, 0:NB, :], ALU.subtract))
                e.tensor_copy(parts[2][:, 0:NB, :], tmp[:, :, :]).then_inc(s_v.sem, 1)
            on("vector")(vec)
            return v

        attr1 = [a[:, :, :].rearrange("p t f -> p (t f)")[:, 0:T] for a in attr]

        def last_of(e, level, width):
            r = rank[:, level, :]
            step(e, e.tensor_scalar(r, r, -1.0, 0.0, ALU.add, ALU.max))
            if level:
                step(e, e.scalar_tensor_tensor(r, rank[:, level - 1, :], float(width), r, ALU.mult, ALU.add))

        def compare(e, entries, blocks, nodes_of, out, room=0):
            shape = [P, blocks, entries.shape[2]]
            hit = carry_hi[:, :, :].rearrange("p b d -> p (b d)")[:, room:room + blocks * shape[2]].rearrange(
                "p (b w) -> p b w", b=blocks)
            ins = tt(e, hit, entries, nodes_of.unsqueeze(2).to_broadcast(shape), ALU.is_le)
            return ins, lambda: e.tensor_reduce(out, hit, AX.X, ALU.add)

        HALF = NB // 2
        found = [k[:, :, :].rearrange("p z e -> p (z e)").bitcast(I32)[:, 0:HALF * W1] for k in hot_key]

        def look_up_start():
            v = bump(s_v)
            per = NB // GROUPS * 2

            def vec(e):
                for b in range(0, NB, per):
                    first, count = compare(e, row_first[:, :].unsqueeze(1).to_broadcast([P, per, W0]), per,
                                           node_id[:, b:b + per], rank[:, 0, b:b + per])
                    step(e, first)
                    step(e, count())
                last_of(e, 0, None)
                e.tensor_copy(rank_i[:, :], rank[:, 0, :]).then_inc(s_v.sem, 1)
            on("vector")(vec)

            def pool(e):
                e.wait_ge(s_v.sem, v)
                for b in range(NB):
                    e.indirect_dma_start(
                        out=found[b // HALF][:, b % HALF * W1:(b % HALF + 1) * W1], out_offset=None,
                        in_=io["pieces"][:, :],
                        in_offset=bass.IndirectOffsetOnAxis(ap=rank_i[:, b:b + 1], axis=0)
                    ).then_inc(s_found.sem, 16)
            on("gpsimd")(pool)

        def look_up_pieces():
            v = bump(s_v)

            def vec(e):
                e.wait_ge(s_found.sem, 16 * NB)
                per = GB
                for k in range(NB // per):
                    b = k * per
                    rows_k = found[b // HALF].rearrange("p (b w) -> p b w", w=W1)[:, b % HALF:b % HALF + per, :]
                    first, count = compare(e, rows_k, per, node_id[:, b:b + per], rank[:, 1, b:b + per])
                    step(e, first)
                    step(e, count())
                last_of(e, 1, W1)
                e.tensor_copy(rank_i[:, :], rank[:, 1, :]).then_inc(s_v.sem, 1)
            on("vector")(vec)
            return v

        def look_up_edges(pieces_ready):
            def chunk(e, i, s):
                cols = bass.ds((i * SLOTS + s) * GB, GB)
                rows_i = G[s][:, 0:GB, 0:W2].bitcast(I32)
                first, count = compare(e, rows_i, GB, node_id[:, cols], rank[:, 2, cols],
                                       s * GB * W2)
                first.then_inc(s_free[s].sem, 1)
                gate(e, "dve", s_free[s], i + (b_free[s] + 1))
                count()
            b_free = [c.n for c in s_free]
            node_gather("look", rank_i, pieces_ready,
                        io["dst"].rearrange("p (k w) -> (p k) w", w=W2).bitcast(F32), W2, [], chunk)
            v = bump(s_v)

            def vec(e):
                step(e, e.memset(sink[:, :], 0.0))
                last_of(e, 2, W2)
                e.tensor_copy(ends_i[:, :], rank[:, 2, :]).then_inc(s_v.sem, 1)
            on("vector")(vec)
            return v

        def nodes(name, is_max, ends_ready):
            run_last = run[(CHUNKS - 1) % SLOTS]
            run_v = s_run[(CHUNKS - 1) % SLOTS].n
            tab = s_tab.n
            p0, v0 = s_p.n, s_v.n
            bump(s_p, 3)
            bump(s_v, 3)

            def vec_carry(e):
                e.wait_ge(s_run[(CHUNKS - 1) % SLOTS].sem, run_v)
                e.tensor_copy(state[:, :], run_last[:, T - 1, :]).then_inc(s_v.sem, 1)
                e.wait_ge(s_p.sem, p0 + 1)
                step(e, e.memset(state_row[:, 0:1], -BIG if is_max else 0.0))
                if is_max:
                    step(e, tt(e, state_row[:, 1:P], pT[0][0:D, 0:P - 1], row_m[:, 0, 1:P], ALU.mult))
                    step(e, tt(e, state_row[:, 1:P], state_row[:, 1:P], row_m[:, 3, 1:P], ALU.add))
                    step(e, e.tensor_tensor_scan(carry_row[:, :], row_m[:, 4, :], state_row[:, :], -BIG,
                                                 ALU.add, ALU.max))
                else:
                    step(e, tt(e, state_row[:, 1:P], pT[0][0:D, 0:P - 1], row_m[:, 0, 1:P], ALU.mult))
                    step(e, e.tensor_tensor_scan(carry_row[:, :], row_m[:, 2, :], state_row[:, :], 0.0,
                                                 ALU.mult, ALU.add))
                e.memset(sink[:, :], 0.0).then_inc(s_v.sem, 1)
                e.wait_ge(s_p.sem, p0 + 2)
                step(e, e.tensor_copy(carry[:, 0:D], pT[1][:, 0:D]))
                e.tensor_tensor(carry_hi[:, :, :], head_hi[:, :].unsqueeze(2).to_broadcast([P, NB, D]),
                                carry[:, 0:D].unsqueeze(1).to_broadcast([P, NB, D]),
                                ALU.mult).then_inc(s_v.sem, 1)
            on("vector")(vec_carry)

            rows_b = [c.n for c in s_rows]

            def pe(e):
                e.wait_ge(s_v.sem, v0 + 1)
                e.transpose(pT[0][0:D, 0:P], state[:, :], ident[:, :]).then_inc(s_p.sem, 1)
                e.wait_ge(s_v.sem, v0 + 2)
                e.transpose(pT[1][:, 0:D], carry_row[:, :], ident[0:D, 0:D]).then_inc(s_p.sem, 1)
                e.wait_ge(s_v.sem, v0 + 3)
                for s in range(SLOTS):
                    e.wait_ge(s_rows[s].sem, rows_b[s])
                flat = carry_hi[:, :, :].rearrange("p b d -> p (b d)")
                w = NB * D // 4
                for k in range(4):
                    e.matmul(pY[k // 2][:, k % 2, 0:w], head_lo[:, :], flat[:, k * w:(k + 1) * w],
                             start=True, stop=True)
                e.matmul(pY[0][:, 2, 0:NB], head_lo[:, :], head_hi[:, :], start=True, stop=True
                         ).then_inc(s_p.sem, 1)
            on("tensor")(pe)

            def chunk(e, i, s):
                flat = agg[:, :, :].rearrange("p b d -> p (b d)")
                e.tensor_copy(flat[:, bass.ds((i * SLOTS + s) * GB * D, GB * D)].rearrange("p (b d) -> p b d", d=D),
                              G[s][:, 0:GB, 0:D]).then_inc(s_free[s].sem, 1)
            node_gather(name, ends_i, ends_ready, scanned, D, [(s_tab, tab)], chunk)

            taken = [c.n for c in s_free]

            def vec_fix(e):
                for s in range(SLOTS):
                    e.wait_ge(s_free[s].sem, taken[s])
                e.wait_ge(s_p.sem, p0 + 3)
                flat = agg[:, :, :].rearrange("p b d -> p (b d)")
                tflat = tmp[:, :, :].rearrange("p b d -> p (b d)")
                w = NB * D // 4
                if is_max:
                    step(e, e.tensor_scalar(stat[:, :], pY[0][:, 2, 0:NB], BIG, -BIG, ALU.mult, ALU.add))
                    for k in range(4):
                        ins = e.tensor_copy(tflat[:, k * w:(k + 1) * w], pY[k // 2][:, k % 2, 0:w])
                    step(e, ins)
                    step(e, tt(e, tmp[:, :, :], tmp[:, :, :], spread(stat[:, :]), ALU.add))
                    step(e, tt(e, agg[:, :, :], agg[:, :, :], tmp[:, :, :], ALU.max))
                else:
                    for k in range(4):
                        ins = tt(e, flat[:, k * w:(k + 1) * w], flat[:, k * w:(k + 1) * w],
                                 pY[k // 2][:, k % 2, 0:w], ALU.add)
                    step(e, ins)
            on("vector")(vec_fix)

        def batch_norm(layer):
            p0, v0, a0 = s_p.n, s_v.n, s_a.n
            bump(s_p, 2)
            bump(s_v, 3)
            bump(s_a)
            per_feature = "p b d -> p d b"

            def pads_to_zero(e, t):
                step(e, e.tensor_scalar(t[:, NB - 1, :], t[:, NB - 1, :], real[:, 0:1], None, ALU.mult))

            def over_blocks(t):
                return t.unsqueeze(1).to_broadcast([P, NB, D])

            def vec(e):
                step(e, tt(e, agg[:, :, :], agg[:, :, :], root[:, :, :], ALU.add))
                pads_to_zero(e, agg)
                e.tensor_reduce(bn[:, 0, :], agg[:, :, :].rearrange(per_feature), AX.X, ALU.add
                                ).then_inc(s_v.sem, 1)
                e.wait_ge(s_p.sem, p0 + 1)
                step(e, e.tensor_scalar(bn[:, 1, :], pT[0][:, 0:D], 1.0 / N, None, ALU.mult))
                step(e, tt(e, agg[:, :, :], agg[:, :, :], over_blocks(bn[:, 1, :]), ALU.subtract))
                pads_to_zero(e, agg)
                step(e, tt(e, tmp[:, :, :], agg[:, :, :], agg[:, :, :], ALU.mult))
                e.tensor_reduce(bn[:, 0, :], tmp[:, :, :].rearrange(per_feature), AX.X, ALU.add
                                ).then_inc(s_v.sem, 1)
                e.wait_ge(s_p.sem, p0 + 2)
                e.tensor_scalar(bn[:, 1, :], pT[0][:, 0:D], 1.0 / N, BN_EPS, ALU.mult, ALU.add
                                ).then_inc(s_v.sem, 1)
                e.wait_ge(s_a.sem, a0 + 1)
                step(e, e.reciprocal(bn[:, 3, :], bn[:, 2, :]))
                step(e, tt(e, bn[:, 3, :], bn[:, 3, :], gamma[:, layer, :], ALU.mult))
                step(e, tt(e, tmp[:, :, :], agg[:, :, :], over_blocks(bn[:, 3, :]), ALU.mult))
                step(e, tt(e, tmp[:, :, :], tmp[:, :, :], over_blocks(beta[:, layer, :]), ALU.add))
                step(e, e.tensor_scalar(h[:, :, :], tmp[:, :, :], 0.0, None, ALU.max))
            on("vector")(vec)

            def pe(e):
                for k in range(2):
                    e.wait_ge(s_v.sem, v0 + 1 + k)
                    e.matmul(pT[0][:, 0:D], ones[:, :], bn[:, 0, :], start=True, stop=True
                             ).then_inc(s_p.sem, 1)
            on("tensor")(pe)

            def act(e):
                e.wait_ge(s_v.sem, v0 + 3)
                e.activation(bn[:, 2, :], bn[:, 1, :], ACT.Sqrt).then_inc(s_a.sem, 1)
            on("scalar")(act)
            publish_h()

        look_up_start()
        norm_relu()
        ends_ready = None
        for layer in range(LAYERS):
            if layer:
                prod = s_prod.n
                nxt = layer

                def load_w(e, prod=prod, nxt=nxt):
                    e.wait_ge(s_prod.sem, prod)
                    e.dma_start(conv_w[:, :], io["conv_w"][nxt]).then_inc(s_w.sem, 16)
                    e.dma_start(edge_w[:, :], io["edge_w"][nxt]).then_inc(s_w.sem, 16)
                on("sync")(load_w)
                bump(s_w, 32)

            def conv_out(e, s, ps, g, k, m):
                e.tensor_copy(rows[s][:, k:k + m, :], ps[:, :, 0:ROW])
                flat = root[:, :, :].rearrange("p b d -> p (b d)")
                return e.tensor_copy(flat[:, bass.ds(g * (GB * D) + k * D, m * D)].rearrange(
                    "p (b d) -> p b d", d=D), ps[:, :, ROW:CW])
            v_parts = parts_of_h()
            node_product(conv_w, CW, conv_out, True,
                         (s_w, s_w.n) if layer else (s_first, FIRST_ALL))
            if layer == 0:
                masks_and_keys()
                pieces_ready = look_up_pieces()
                keyed = first_hots("conv0")
            edges(f"conv{layer}", conv_table, ROW, io["attr"], EF, [(s_tab, s_tab.n)], False,
                  v_parts, keyed)
            keyed = first_hots(f"after{layer}")
            if layer == 0:
                ends_ready = look_up_edges(pieces_ready)
            nodes(f"end{layer}", False, ends_ready)
            if layer < LAYERS - 1:
                batch_norm(layer)
            else:
                def last_relu(e):
                    step(e, tt(e, agg[:, :, :], agg[:, :, :], root[:, :, :], ALU.add))
                    step(e, e.tensor_scalar(h[:, :, :], agg[:, :, :], 0.0, None, ALU.max))
                on("vector")(last_relu)
                publish_h()

        def residual_out(e, s, ps, g, k, m):
            flat = x[:, :, :].rearrange("p b d -> p (b d)")
            there = flat[:, bass.ds(g * (GB * D), GB * D)]
            return e.tensor_tensor(there, there, ps.rearrange("p b c -> p (b c)"), ALU.add)

        node_product(lin_w[:, 0, :], D, residual_out, False)
        all_rows = [c.n for c in s_rows]

        def order_x(e):
            for s in range(SLOTS):
                e.wait_ge(s_rows[s].sem, all_rows[s])
        on("vector")(order_x)

        norm_relu()
        h_ready = s_v.n
        v_parts = parts_of_h()
        max_stored = sem("s_max_table")

        def store_h(e):
            e.wait_ge(s_v.sem, h_ready)
            e.dma_start(max_table.rearrange("(b p) c -> p b c", p=P), h[:, :, :]).then_inc(max_stored.sem, 16)
        on("sync")(store_h)

        def to_max(e):
            step(e, e.tensor_scalar(same[:, :], same[:, :], BIG, -BIG, ALU.mult, ALU.add))
        on("vector")(to_max)
        edges("max", max_table, D, io["weight"], 1, [(max_stored, 16)], True, v_parts, keyed)
        nodes("end_max", True, ends_ready)

        def take_agg(e):
            step(e, e.tensor_copy(h[:, :, :], agg[:, :, :]))
        on("vector")(take_agg)
        publish_h()
        node_product(lin_w[:, 1, :], D, residual_out, False)
        done = [c.n for c in s_rows]

        def write_out(e):
            for s in range(SLOTS):
                e.wait_ge(s_rows[s].sem, done[s])
            e.dma_start(io["out"], x[:, :, :]).then_inc(s_out.sem, 16)
            e.wait_ge(s_out.sem, 16)
        on("sync")(write_out)

        block = ctx.enter_context(nc.Block())

        def attach(decorate, name):
            @decorate
            def _(e):
                for f in programs[name]:
                    f(e)
        attach(block.sync, "sync")
        attach(block.gpsimd, "gpsimd")
        attach(block.scalar, "scalar")
        attach(block.vector, "vector")
        attach(block.tensor, "tensor")


def kernel(**inputs):
    import concourse.bacc as _bacc
    from concourse.bass_utils import run_bass_kernel_spmd as _run

    def streams(a, fill):
        a = np.asarray(a).reshape(E, -1)
        out = np.full((EPAD, a.shape[1]), fill, a.dtype)
        out[:E] = a
        return out.reshape(P, -1)

    def diagonal(n, blocks, width, bias):
        out = np.zeros((n * D + 1, n * width), np.float32)
        for b in range(n):
            out[b * D:(b + 1) * D, b * width:(b + 1) * width] = blocks
            out[n * D, b * width:(b + 1) * width] = bias
        return out

    f = {k: np.asarray(v) for k, v in inputs.items()}
    dst = streams(f["dst"], NPAD - 1)
    first, last = dst[:, 0], dst[:, -1]
    none = np.full(1, -1, dst.dtype)
    prev_last, prev_first = np.concatenate([none, last[:-1]]), np.concatenate([none, first[:-1]])
    next_first = np.concatenate([first[1:], none])

    x = np.zeros((NPAD, D), np.float32)
    x[:N] = f["x"]
    conv_w, edge_w = [], []
    for layer in range(LAYERS):
        ew = f["L0_gnn_edge_w"][layer].reshape(EF, D, D).transpose(1, 0, 2).reshape(D, EF * D)
        eb = f["L0_gnn_edge_b"][layer].reshape(D, D)
        block = np.concatenate([ew, eb, f["L0_gnn_root_w"][layer]], axis=1)
        bias = np.concatenate([np.zeros(ROW, np.float32), f["L0_gnn_root_b"][layer]])
        conv_w.append(diagonal(GB, block, CW, bias))
        edge_w.append(diagonal(TP, block[:, :ROW], ROW, bias[:ROW])[:-1])
    lin_w = np.stack([diagonal(GB, f["L0_gnn_pred_w"], D, f["L0_gnn_pred_b"]),
                      diagonal(GB, f["L1_gnn_W"].T, D, f["L1_gnn_b"])], axis=1)
    order = np.arange(P)
    arrays = {
        "src": streams(f["src"], 0), "dst": dst, "attr": streams(f["edge_attr_8"], 0),
        "weight": streams(f["edge_weight1"], 0),
        "x": x.reshape(NB, P, D).transpose(1, 0, 2),
        "ident": np.eye(P, dtype=np.float32),
        "node_id": (order[:, None] + P * np.arange(NB)).astype(np.float32),
        "row_first": np.broadcast_to(dst.reshape(-1)[::W1 * W2], (P, W0)),
        "pieces": dst.reshape(-1)[::W2].reshape(W0, W1),
        "edge_w": np.stack(edge_w),
        "zone_lane": (order[:, None] + P * np.arange(ZONES)).astype(np.float32),
        "near_mask": np.eye(NEAR, dtype=np.float32).astype(mybir.dt.np(BF16))[:, :, None].repeat(D, 2),
        "pe_src": streams(f["src"], 0).reshape(P, CHUNKS, T)[:, :, TG:].transpose(1, 2, 0).reshape(
            CHUNKS, PE_EDGES),
        "lanes": np.broadcast_to(order.astype(np.float32), (P, P)),
        "real": (order < LAST).astype(np.float32)[:, None],
        "lin_w": lin_w, "conv_w": np.stack(conv_w),
        "gamma": np.broadcast_to(f["L0_gnn_bn_gamma"], (P, LAYERS - 1, D)),
        "beta": np.broadcast_to(f["L0_gnn_bn_beta"], (P, LAYERS - 1, D)),
        "borders": np.stack([first, last, prev_last, next_first], axis=1),
        "borders_row": np.broadcast_to(np.stack([first, prev_last, prev_first]), (D, 3, P)),
    }
    nc = _bacc.Bacc("TRN2", target_bir_lowering=False, num_devices=1)
    arrays = {f"in_{k}": np.ascontiguousarray(v) for k, v in arrays.items()}
    io = {k[3:]: nc.dram_tensor(k, v.shape, mybir.dt.from_np(v.dtype), kind="ExternalInput").ap()
          for k, v in arrays.items()}
    io["out"] = nc.dram_tensor("out", (P, NB, D), F32, kind="ExternalOutput").ap()
    build(nc, io)
    got = _run(nc, [arrays], core_ids=[0]).results[0]["out"]
    return np.asarray(got).transpose(1, 0, 2).reshape(NPAD, D)[:N]
```
